# Optimizing a Trainium2 kernel written in Bass

```python
import numpy as np
import jax
import jax.numpy as jnp

def _softmax(x, axis=-1):
    return jax.nn.softmax(x, axis=axis)

def _gelu(x):
    return jax.nn.gelu(x, approximate=True)

def _silu(x):
    return jax.nn.silu(x)

def _sigmoid(x):
    return jax.nn.sigmoid(x)

def _layernorm(x, axis=-1, eps=1e-05):
    m = jnp.mean(x, axis=axis, keepdims=True)
    v = jnp.var(x, axis=axis, keepdims=True)
    return (x - m) / jnp.sqrt(v + eps)

def _scatter_add(tgt, idx, src, axis=0):
    return tgt.at[idx].add(src)

def _segment_sum(src, seg, n):
    return jax.ops.segment_sum(src, seg, n)
kernel_name = 'mk_conv_seq_d2_conv_nchw256_r2_a0c261'

def setup_inputs(seed: int=0):
    np.random.seed(seed)
    _w = jnp.asarray

    def _rec_inputs():
        import jax
        import jax.numpy as jnp
        _gk = jax.random.key(seed)
        x = -0.000125 + 0.9999 * jax.random.normal(jax.random.fold_in(_gk, 1), (8, 128, 64, 64), jnp.float32)
        return x
    x = _rec_inputs()

    def _L0_conv_setup():
        import jax, jax.numpy as jnp
        import numpy as np
        WIN = 8
        HEADS = 8
        DOWN = 4
        STRIDE = WIN // DOWN
        LEVELS = len([i for i in range(8) if WIN / DOWN ** i >= 1])
        EPS = 1e-05

        def circular_pad(x, pad_r, pad_b):
            N, H, W, C = x.shape
            Hr = -(-(H + pad_b) // H)
            Wr = -(-(W + pad_r) // W)
            return jnp.tile(x, (1, Hr, Wr, 1))[:, :H + pad_b, :W + pad_r, :]

        def pad_fit_win(x, ws):
            N, H, W, C = x.shape
            H_ = -(-H // ws) * ws
            W_ = -(-W // ws) * ws
            return circular_pad(x, W_ - W, H_ - H)

        def window_partition(x, ws):
            N, H, W, C = x.shape
            x = x.reshape(N, H // ws, ws, W // ws, ws, C)
            return x.transpose(0, 1, 3, 2, 4, 5).reshape(-1, ws, ws, C)

        def window_reverse(w, ws, H, W):
            B = w.shape[0] // (H // ws * (W // ws))
            x = w.reshape(B, H // ws, W // ws, ws, ws, -1)
            return x.transpose(0, 1, 3, 2, 4, 5).reshape(B, H, W, -1)

        def layernorm(x, g, b):
            mu = jnp.mean(x, -1, keepdims=True)
            var = jnp.var(x, -1, keepdims=True)
            return (x - mu) * jax.lax.rsqrt(var + EPS) * g + b

        def mha(q, k, v, wq, wk, wv, wf, bf):
            B, Lq, C = q.shape
            Lk = k.shape[1]
            dh = C // HEADS
            qh = (q @ wq).reshape(B, Lq, HEADS, dh)
            kh = (k @ wk).reshape(B, Lk, HEADS, dh)
            vh = (v @ wv).reshape(B, Lk, HEADS, dh)
            attn = jnp.einsum('bqhd,bkhd->bhqk', qh, kh) * (1.0 / dh ** 0.5)
            attn = jax.nn.softmax(attn, axis=-1)
            o = jnp.einsum('bhqk,bkhd->bqhd', attn, vh).reshape(B, Lq, C)
            return o @ wf + bf

        def self_attention(x, wq, wk, wv, wf, bf):
            N, H, W, C = x.shape
            xp = pad_fit_win(x, WIN)
            _, H_, W_, _ = xp.shape
            xw = window_partition(xp, WIN).reshape(-1, WIN * WIN, C)
            res = mha(xw, xw, xw, wq, wk, wv, wf, bf)
            res = window_reverse(res.reshape(-1, WIN, WIN, C), WIN, H_, W_)
            return (xp + res)[:, :H, :W, :]

        def cross_attention(q, kv, wq, wk, wv, wf, bf):
            N, qH, qW, C = q.shape
            _, kH, kW, _ = kv.shape
            qp = pad_fit_win(q, WIN)
            _, qH_, qW_, _ = qp.shape
            qw = window_partition(qp, WIN).reshape(-1, WIN * WIN, C)
            kH_ = (-(-kH // STRIDE) - 1) * STRIDE + WIN
            kW_ = (-(-kW // STRIDE) - 1) * STRIDE + WIN
            kvp = circular_pad(kv, kW_ - kW, kH_ - kH)
            nH = (kH_ - WIN) // STRIDE + 1
            nW = (kW_ - WIN) // STRIDE + 1
            ri = (jnp.arange(nH) * STRIDE)[:, None] + jnp.arange(WIN)
            ci = (jnp.arange(nW) * STRIDE)[:, None] + jnp.arange(WIN)
            patches = kvp[:, ri][:, :, :, ci]
            patches = patches.transpose(0, 1, 3, 2, 4, 5).reshape(-1, WIN * WIN, C)
            res = mha(qw, patches, patches, wq, wk, wv, wf, bf)
            res = window_reverse(res.reshape(-1, WIN, WIN, C), WIN, qH_, qW_)
            return (qp + res)[:, :qH, :qW, :]

        def avgpool4(x):
            N, H, W, C = x.shape
            return x.reshape(N, H // DOWN, DOWN, W // DOWN, DOWN, C).mean((2, 4))
        key = jax.random.key(seed)
        ks = jax.random.split(key, 12)
        D, DF = (128, 512)
        N, H, W = (8, 64, 64)
        s = 0.02

        def w(k, shape):
            return jax.random.normal(k, shape, jnp.float32) * s
        return {'x': jax.random.normal(ks[0], (N, D, H, W), jnp.float32), 'sa_wq': w(ks[1], (D, D)), 'sa_wk': w(ks[2], (D, D)), 'sa_wv': w(ks[3], (D, D)), 'sa_wf': w(ks[4], (D, D)), 'sa_bf': jnp.zeros((D,), jnp.float32), 'ca_wq': w(ks[5], (D, D)), 'ca_wk': w(ks[6], (D, D)), 'ca_wv': w(ks[7], (D, D)), 'ca_wf': w(ks[8], (D, D)), 'ca_bf': jnp.zeros((D,), jnp.float32), 'ln_self_g': jnp.ones((D,), jnp.float32), 'ln_self_b': jnp.zeros((D,), jnp.float32), 'ln_cross_g': jnp.ones((D,), jnp.float32), 'ln_cross_b': jnp.zeros((D,), jnp.float32), 'ffn_w1': w(ks[9], (D, DF)), 'ffn_b1': jnp.zeros((DF,), jnp.float32), 'ffn_w2': w(ks[10], (DF, D)), 'ffn_b2': jnp.zeros((D,), jnp.float32), 'ln_out_g': jnp.ones((D,), jnp.float32), 'ln_out_b': jnp.zeros((D,), jnp.float32)}
    _L0_conv_all = _L0_conv_setup()
    _L0_conv_in = {k: v for k, v in _L0_conv_all.items() if k in ('sa_wq', 'sa_wk', 'sa_wv', 'sa_wf', 'sa_bf', 'ca_wq', 'ca_wk', 'ca_wv', 'ca_wf', 'ca_bf', 'ln_self_g', 'ln_self_b', 'ln_cross_g', 'ln_cross_b', 'ffn_w1', 'ffn_b1', 'ffn_w2', 'ffn_b2', 'ln_out_g', 'ln_out_b')}
    del _L0_conv_all

    def _L1_conv_setup():
        import jax, jax.numpy as jnp
        from jax import lax
        import numpy as np
        EPS = 1e-05
        HT_LIM = 1.3

        def _binarize_ste(t):
            return t + lax.stop_gradient(jnp.sign(t) - t)
        key = jax.random.key(seed)
        k1, k2, k3 = jax.random.split(key, 3)
        C = 128
        x = jax.random.normal(k1, (32, C, 56, 56), dtype=jnp.float32)
        weight = jax.random.normal(k2, (C, C, 3, 3), dtype=jnp.float32) * 0.05
        gamma = jnp.ones((C,), dtype=jnp.float32)
        beta = jnp.zeros((C,), dtype=jnp.float32)
        return {'x': x, 'weight': weight, 'gamma': gamma, 'beta': beta}
    _L1_conv_all = _L1_conv_setup()
    _L1_conv_in = {k: v for k, v in _L1_conv_all.items() if k in ('weight', 'gamma', 'beta')}
    del _L1_conv_all
    return {'x': x, 'L0_conv_sa_wq': _L0_conv_in['sa_wq'], 'L0_conv_sa_wk': _L0_conv_in['sa_wk'], 'L0_conv_sa_wv': _L0_conv_in['sa_wv'], 'L0_conv_sa_wf': _L0_conv_in['sa_wf'], 'L0_conv_sa_bf': _L0_conv_in['sa_bf'], 'L0_conv_ca_wq': _L0_conv_in['ca_wq'], 'L0_conv_ca_wk': _L0_conv_in['ca_wk'], 'L0_conv_ca_wv': _L0_conv_in['ca_wv'], 'L0_conv_ca_wf': _L0_conv_in['ca_wf'], 'L0_conv_ca_bf': _L0_conv_in['ca_bf'], 'L0_conv_ln_self_g': _L0_conv_in['ln_self_g'], 'L0_conv_ln_self_b': _L0_conv_in['ln_self_b'], 'L0_conv_ln_cross_g': _L0_conv_in['ln_cross_g'], 'L0_conv_ln_cross_b': _L0_conv_in['ln_cross_b'], 'L0_conv_ffn_w1': _L0_conv_in['ffn_w1'], 'L0_conv_ffn_b1': _L0_conv_in['ffn_b1'], 'L0_conv_ffn_w2': _L0_conv_in['ffn_w2'], 'L0_conv_ffn_b2': _L0_conv_in['ffn_b2'], 'L0_conv_ln_out_g': _L0_conv_in['ln_out_g'], 'L0_conv_ln_out_b': _L0_conv_in['ln_out_b'], 'L1_conv_weight': _L1_conv_in['weight'], 'L1_conv_gamma': _L1_conv_in['gamma'], 'L1_conv_beta': _L1_conv_in['beta']}

def reference(x, L0_conv_sa_wq, L0_conv_sa_wk, L0_conv_sa_wv, L0_conv_sa_wf, L0_conv_sa_bf, L0_conv_ca_wq, L0_conv_ca_wk, L0_conv_ca_wv, L0_conv_ca_wf, L0_conv_ca_bf, L0_conv_ln_self_g, L0_conv_ln_self_b, L0_conv_ln_cross_g, L0_conv_ln_cross_b, L0_conv_ffn_w1, L0_conv_ffn_b1, L0_conv_ffn_w2, L0_conv_ffn_b2, L0_conv_ln_out_g, L0_conv_ln_out_b, L1_conv_weight, L1_conv_gamma, L1_conv_beta):
    import jax
    import jax.numpy as jnp

    def _L0_conv_ref(x, sa_wq, sa_wk, sa_wv, sa_wf, sa_bf, ca_wq, ca_wk, ca_wv, ca_wf, ca_bf, ln_self_g, ln_self_b, ln_cross_g, ln_cross_b, ffn_w1, ffn_b1, ffn_w2, ffn_b2, ln_out_g, ln_out_b):
        import jax, jax.numpy as jnp
        import numpy as np
        WIN = 8
        HEADS = 8
        DOWN = 4
        STRIDE = WIN // DOWN
        LEVELS = len([i for i in range(8) if WIN / DOWN ** i >= 1])
        EPS = 1e-05

        def circular_pad(x, pad_r, pad_b):
            N, H, W, C = x.shape
            Hr = -(-(H + pad_b) // H)
            Wr = -(-(W + pad_r) // W)
            return jnp.tile(x, (1, Hr, Wr, 1))[:, :H + pad_b, :W + pad_r, :]

        def pad_fit_win(x, ws):
            N, H, W, C = x.shape
            H_ = -(-H // ws) * ws
            W_ = -(-W // ws) * ws
            return circular_pad(x, W_ - W, H_ - H)

        def window_partition(x, ws):
            N, H, W, C = x.shape
            x = x.reshape(N, H // ws, ws, W // ws, ws, C)
            return x.transpose(0, 1, 3, 2, 4, 5).reshape(-1, ws, ws, C)

        def window_reverse(w, ws, H, W):
            B = w.shape[0] // (H // ws * (W // ws))
            x = w.reshape(B, H // ws, W // ws, ws, ws, -1)
            return x.transpose(0, 1, 3, 2, 4, 5).reshape(B, H, W, -1)

        def layernorm(x, g, b):
            mu = jnp.mean(x, -1, keepdims=True)
            var = jnp.var(x, -1, keepdims=True)
            return (x - mu) * jax.lax.rsqrt(var + EPS) * g + b

        def mha(q, k, v, wq, wk, wv, wf, bf):
            B, Lq, C = q.shape
            Lk = k.shape[1]
            dh = C // HEADS
            qh = (q @ wq).reshape(B, Lq, HEADS, dh)
            kh = (k @ wk).reshape(B, Lk, HEADS, dh)
            vh = (v @ wv).reshape(B, Lk, HEADS, dh)
            attn = jnp.einsum('bqhd,bkhd->bhqk', qh, kh) * (1.0 / dh ** 0.5)
            attn = jax.nn.softmax(attn, axis=-1)
            o = jnp.einsum('bhqk,bkhd->bqhd', attn, vh).reshape(B, Lq, C)
            return o @ wf + bf

        def self_attention(x, wq, wk, wv, wf, bf):
            N, H, W, C = x.shape
            xp = pad_fit_win(x, WIN)
            _, H_, W_, _ = xp.shape
            xw = window_partition(xp, WIN).reshape(-1, WIN * WIN, C)
            res = mha(xw, xw, xw, wq, wk, wv, wf, bf)
            res = window_reverse(res.reshape(-1, WIN, WIN, C), WIN, H_, W_)
            return (xp + res)[:, :H, :W, :]

        def cross_attention(q, kv, wq, wk, wv, wf, bf):
            N, qH, qW, C = q.shape
            _, kH, kW, _ = kv.shape
            qp = pad_fit_win(q, WIN)
            _, qH_, qW_, _ = qp.shape
            qw = window_partition(qp, WIN).reshape(-1, WIN * WIN, C)
            kH_ = (-(-kH // STRIDE) - 1) * STRIDE + WIN
            kW_ = (-(-kW // STRIDE) - 1) * STRIDE + WIN
            kvp = circular_pad(kv, kW_ - kW, kH_ - kH)
            nH = (kH_ - WIN) // STRIDE + 1
            nW = (kW_ - WIN) // STRIDE + 1
            ri = (jnp.arange(nH) * STRIDE)[:, None] + jnp.arange(WIN)
            ci = (jnp.arange(nW) * STRIDE)[:, None] + jnp.arange(WIN)
            patches = kvp[:, ri][:, :, :, ci]
            patches = patches.transpose(0, 1, 3, 2, 4, 5).reshape(-1, WIN * WIN, C)
            res = mha(qw, patches, patches, wq, wk, wv, wf, bf)
            res = window_reverse(res.reshape(-1, WIN, WIN, C), WIN, qH_, qW_)
            return (qp + res)[:, :qH, :qW, :]

        def avgpool4(x):
            N, H, W, C = x.shape
            return x.reshape(N, H // DOWN, DOWN, W // DOWN, DOWN, C).mean((2, 4))
        N, C, H, W = x.shape
        xh = x.transpose(0, 2, 3, 1)
        xh = pad_fit_win(xh, WIN)
        attn_list = []
        for idx in range(LEVELS):
            xa = self_attention(xh, sa_wq, sa_wk, sa_wv, sa_wf, sa_bf)
            xa = layernorm(xa, ln_self_g, ln_self_b)
            attn_list.append(xa)
            if idx < LEVELS - 1:
                xh = avgpool4(xa)
        kv = attn_list[-1]
        for idx in range(LEVELS - 1, 0, -1):
            q = cross_attention(attn_list[idx - 1], kv, ca_wq, ca_wk, ca_wv, ca_wf, ca_bf)
            q = layernorm(q, ln_cross_g, ln_cross_b)
            kv = q
        q = kv[:, :H, :W, :]
        res = jax.nn.relu(q @ ffn_w1 + ffn_b1) @ ffn_w2 + ffn_b2
        out = layernorm(q + res, ln_out_g, ln_out_b)
        return out.transpose(0, 3, 1, 2)

    def _L1_conv_ref(x, weight, gamma, beta):
        import jax, jax.numpy as jnp
        from jax import lax
        import numpy as np
        EPS = 1e-05
        HT_LIM = 1.3

        def _binarize_ste(t):
            return t + lax.stop_gradient(jnp.sign(t) - t)
        xt = jnp.clip(x, -HT_LIM, HT_LIM)
        xb = _binarize_ste(xt)
        wb = _binarize_ste(weight)
        y = lax.conv_general_dilated(xb, wb, window_strides=(1, 1), padding=((1, 1), (1, 1)), dimension_numbers=('NCHW', 'OIHW', 'NCHW'))
        mean = jnp.mean(y, axis=(0, 2, 3), keepdims=True)
        var = jnp.mean(jnp.square(y - mean), axis=(0, 2, 3), keepdims=True)
        y = (y - mean) * lax.rsqrt(var + EPS)
        y = y * gamma[None, :, None, None] + beta[None, :, None, None]
        return x + y

    def _gn(v, G=32, eps=1e-05):
        B_, C_, H_, W_ = v.shape
        g = v.reshape(B_, G, C_ // G, H_, W_)
        m = jnp.mean(g, axis=(2, 3, 4), keepdims=True)
        s = jnp.var(g, axis=(2, 3, 4), keepdims=True)
        return ((g - m) / jnp.sqrt(s + eps)).reshape(v.shape)

    def _ln_c(v, eps=1e-06):
        m = jnp.mean(v, axis=1, keepdims=True)
        s = jnp.var(v, axis=1, keepdims=True)
        return (v - m) / jnp.sqrt(s + eps)

    def _ln_t(v, eps=1e-05):
        m = jnp.mean(v, axis=-1, keepdims=True)
        s = jnp.var(v, axis=-1, keepdims=True)
        return (v - m) / jnp.sqrt(s + eps)

    def _to_tokens(v):
        B_, C_, H_, W_ = v.shape
        return v.reshape(B_, C_, H_ * W_).transpose(0, 2, 1)

    def _from_tokens(t, like):
        B_, C_, H_, W_ = like.shape
        return t.transpose(0, 2, 1).reshape(B_, C_, H_, W_)
    x = _L0_conv_ref(x, L0_conv_sa_wq, L0_conv_sa_wk, L0_conv_sa_wv, L0_conv_sa_wf, L0_conv_sa_bf, L0_conv_ca_wq, L0_conv_ca_wk, L0_conv_ca_wv, L0_conv_ca_wf, L0_conv_ca_bf, L0_conv_ln_self_g, L0_conv_ln_self_b, L0_conv_ln_cross_g, L0_conv_ln_cross_b, L0_conv_ffn_w1, L0_conv_ffn_b1, L0_conv_ffn_w2, L0_conv_ffn_b2, L0_conv_ln_out_g, L0_conv_ln_out_b)
    x = _L1_conv_ref(x, L1_conv_weight, L1_conv_gamma, L1_conv_beta)
    return x

_drawn_inputs = setup_inputs


def setup_inputs(seed=0):
    import zlib

    import numpy as np

    out = dict(_drawn_inputs(seed))
    spreads = {'L0_conv_sa_bf': (0.0, 0.1),
     'L0_conv_ca_bf': (0.0, 0.1),
     'L0_conv_ln_self_g': (1.0, 0.2),
     'L0_conv_ln_self_b': (0.0, 0.1),
     'L0_conv_ln_cross_g': (1.0, 0.2),
     'L0_conv_ln_cross_b': (0.0, 0.1),
     'L0_conv_ffn_b1': (0.0, 0.1),
     'L0_conv_ffn_b2': (0.0, 0.1),
     'L0_conv_ln_out_g': (1.0, 0.2),
     'L0_conv_ln_out_b': (0.0, 0.1),
     'L1_conv_gamma': (1.0, 0.2),
     'L1_conv_beta': (0.0, 0.1)}
    factors = {'L0_conv_sa_wq': 4.158,
     'L0_conv_sa_wk': 4.196,
     'L0_conv_ca_wq': 4.722,
     'L0_conv_ca_wk': 4.757}
    for name, (base, spread) in spreads.items():
        noise = np.random.default_rng([zlib.crc32(name.encode()), seed]).standard_normal(out[name].shape)
        drawn = base * np.exp(spread * noise) if base else spread * noise
        out[name] = jnp.asarray(drawn.astype(out[name].dtype))
    for name, factor in factors.items():
        out[name] = (out[name] * factor).astype(out[name].dtype)
    return out
```

```python
from contextlib import ExitStack
from collections import namedtuple

import concourse.bass as bass
from concourse import mybir

ALU = mybir.AluOpType
ACT = mybir.ActivationFunctionType
AX = mybir.AxisListType
F32 = mybir.dt.float32
F16 = mybir.dt.float16
BF16 = mybir.dt.bfloat16

IMAGES, C, H, W = 8, 128, 64, 64
WIN = 8
TOK = WIN * WIN
HEADS = 8
DH = C // HEADS
STRIPS = H // WIN
SW = WIN * W
PAIRS = SW // (2 * TOK)
DOWN = 4
LH = H // DOWN
LT = LH * LH
LPAIRS = LT // (2 * TOK)
STRIDE = WIN // DOWN
KP = LH - STRIDE + WIN
DF = 512
FB = DF // C
VC = 96
MAP = W + 2
TAPS = 9
EPS = 1e-5
QS = DH ** -0.5
CHUNK = 1024
CHUNKS = H * W // CHUNK
PER = STRIPS // 2

Unit = namedtuple("Unit", "kind half par no pairs body crosses first")


def attention_conv(nc, x, wq, wk, wv, wf, bias_rows, gains, shifts, b1, w1, w2, convw, bn, consts, out):
    with ExitStack() as ctx:
        def sb(name, shape, dt=F32):
            return ctx.enter_context(nc.sbuf_tensor(name, shape, dt))

        def bank(name):
            return ctx.enter_context(nc.psum_tensor(name, [128, 512], F32))

        def sem(name):
            return ctx.enter_context(nc.semaphore(name))

        self_out = nc.dram_tensor("self_out", (IMAGES * STRIPS, C, SW), F32, kind="Internal").ap()
        ffn_out = nc.dram_tensor("ffn_out", (IMAGES, C, H * W), F32, kind="Internal").ap()

        wq_sb, wk_sb, wv_sb, wf_sb = (sb(n, [128, 2, C]) for n in ("wq_sb", "wk_sb", "wv_sb", "wf_sb"))
        w1_sb = sb("w1_sb", [128, DF])
        w2_sb = sb("w2_sb", [128, FB, C])
        b1_sb = sb("b1_sb", [128, FB])
        gain = sb("gain", [128, 3])
        shift = sb("shift", [128, 3])
        bn_sb = sb("bn_sb", [128, 2])
        convs = sb("convs", [128, TAPS, C], BF16)
        ident = sb("ident", [128, 128])
        headmask = sb("headmask", [128, 4])
        identb = sb("identb", [128, 128], BF16)
        ones2_f = sb("ones2_f", [2, 128])
        ones2 = sb("ones2", [2, 128], F16)
        brow_f = sb("brow_f", [1, 3 * C])
        brow_hi = sb("brow_hi", [1, 3 * C], F16)
        brow_lo = sb("brow_lo", [1, 3 * C], F16)
        brow = sb("brow", [2, 3, PAIRS, C], F16)
        half_neg = sb("half_neg", [128, PAIRS])
        eps = sb("eps", [128, PAIRS])

        xself = sb("xself", [128, 2, SW])
        xcross = sb("xcross", [128, 2, SW])
        xpatch = sb("xpatch", [128, 2, SW])
        xlow = sb("xlow", [128, LT])
        qc_hi = sb("qc_hi", [128, 8 * TOK], F16)
        qc_lo = sb("qc_lo", [128, 8 * TOK], F16)
        qm_hi = sb("qm_hi", [128, 2, 8, 4, TOK], F16)
        qm_lo = sb("qm_lo", [128, 2, 8, 4, TOK], F16)
        ks_hi = sb("ks_hi", [128, 2, 8, 2, TOK], F16)
        ks_lo = sb("ks_lo", [128, 2, 8, 2, TOK], F16)
        vb = sb("vb", [128, 2, PAIRS * 4, VC])
        negmax = sb("negmax", [128, 2, 8], BF16)
        negmax_b = sb("negmax_b", [128, 2, 8, TOK], BF16)
        prob = sb("prob", [128, 2, 512])
        rden = sb("rden", [128, 2, 4, 2])
        onorm = sb("onorm", [128, 2, PAIRS, C])
        oT = sb("oT", [128, SW])
        stats = sb("stats", [128, PAIRS, 6])
        mv = sb("mv", [128, PAIRS, 2])
        vareps = sb("vareps", [128, PAIRS])
        rstd = sb("rstd", [128, PAIRS])
        xn = sb("xn", [128, SW])
        xa = sb("xa", [128, 2, SW])
        colsum = sb("colsum", [128, SW // DOWN])
        low_sum = sb("low_sum", [128, STRIPS, 32])
        low_out = sb("low_out", [128, LT])
        kvpad = sb("kvpad", [128, KP, KP])
        xf = sb("xf", [128, SW])
        hid = sb("hid", [128, FB, SW])
        x2 = sb("x2", [128, 2, SW])
        smap = sb("smap", [128, MAP, MAP], BF16)
        yconv = sb("yconv", [128, IMAGES * H * W], F16)
        ystats = sb("ystats", [128, IMAGES * STRIPS, 6])
        bnv = sb("bnv", [128, 8])
        lastx = sb("lastx", [128, CHUNKS, CHUNK])
        lasty = sb("lasty", [128, 2, CHUNK])

        ps_proj, ps_hid, ps_max, ps_o, ps_t, ps_y = (
            bank(n) for n in ("ps_proj", "ps_hid", "ps_max", "ps_o", "ps_t", "ps_y"))
        ps_s = [bank("ps_s0"), bank("ps_s1")]

        s_setup = sem("s_setup")
        s_brow = sem("s_brow")
        s_xself_in = [sem("s_xself_in0"), sem("s_xself_in1")]
        s_xcross = [sem("s_xcross0"), sem("s_xcross1")]
        s_self_stored = [sem("s_self_stored0"), sem("s_self_stored1")]
        s_x2_stored = [sem("s_x2_stored0"), sem("s_x2_stored1")]
        s_last_in = [sem(f"s_last_in{q}") for q in range(CHUNKS)]
        s_last_out = [sem(f"s_last_out{q}") for q in range(CHUNKS)]
        s_prep_v = sem("s_prep_v")
        s_prep_a = sem("s_prep_a")
        s_prep_g = sem("s_prep_g")
        s_xpatch = sem("s_xpatch")
        s_rstd = sem("s_rstd")
        s_rstd2 = sem("s_rstd2")
        s_q = sem("s_q")
        s_k = sem("s_k")
        s_v = sem("s_v")
        s_proj_free = sem("s_proj_free")
        s_qhi = sem("s_qhi")
        s_qm = sem("s_qm")
        s_khi = sem("s_khi")
        s_ot = sem("s_ot")
        s_oT = sem("s_oT")
        s_y = sem("s_y")
        s_stats = sem("s_stats")
        s_mv = sem("s_mv")
        s_var = sem("s_var")
        s_aggr = sem("s_aggr")
        s_xn = sem("s_xn")
        s_xt = sem("s_xt")
        s_xt_out = sem("s_xt_out")
        s_max = sem("s_max")
        s_neg = sem("s_neg")
        s_negb = sem("s_negb")
        s_s = sem("s_s")
        s_prob = sem("s_prob")
        s_pv = sem("s_pv")
        s_rden = sem("s_rden")
        s_on = sem("s_on")
        s_hid = sem("s_hid")
        s_relu = sem("s_relu")
        s_y2 = sem("s_y2")
        s_stats2 = sem("s_stats2")
        s_mv2 = sem("s_mv2")
        s_var2 = sem("s_var2")
        s_xn2 = sem("s_xn2")
        s_xt2 = sem("s_xt2")
        s_x2 = sem("s_x2")
        s_sign = sem("s_sign")
        s_colsum = sem("s_colsum")
        s_pooled = sem("s_pooled")
        s_xlow = sem("s_xlow")
        s_kv0 = sem("s_kv0")
        s_kv1 = sem("s_kv1")
        s_kv = sem("s_kv")
        s_conv = sem("s_conv")
        s_yconv = sem("s_yconv")
        s_ystats = sem("s_ystats")
        s_bn = sem("s_bn")
        s_bnr = sem("s_bnr")
        s_bnab = sem("s_bnab")
        s_affine = sem("s_affine")
        s_sum = sem("s_sum")

        def unit(kind, half, par, no, body, crosses, first):
            return Unit(kind, half, par, no, LPAIRS if kind == "low" else PAIRS, body, crosses, first)

        def walk(fori, body, section):
            with fori(0, PER) as i:
                body([unit("self", h, h, i * 2 + h, i, 0, h == 0) for h in range(2)], 0, i)
            section(unit("low", 0, 0, STRIPS, 0, 0, True), None)
            per_image = 2 * STRIPS + 1
            with fori(0, IMAGES - 1) as n:
                with fori(0, PER) as i:
                    no = n * per_image + i * 4 + (STRIPS + 1)
                    bc = n * PER + i
                    body([unit("cross" if u % 2 == 0 else "self", u // 2, u % 2, no + u,
                               bc if u % 2 == 0 else bc + PER, bc * 2 + (u + 1) // 2, u == 0)
                          for u in range(4)], n, i)
                section(unit("low", 0, 0, n * per_image + (3 * STRIPS + 1), n + 1, n * STRIPS + STRIPS, True), n)
            with fori(0, PER) as i:
                no = i * 2 + (STRIPS + 1 + (IMAGES - 1) * per_image)
                bc = i + (IMAGES - 1) * PER
                body([unit("cross", h, h, no + h, bc, bc * 2 + h, h == 0) for h in range(2)], IMAGES - 1, i)
            section(None, IMAGES - 1)

        def slots(body_units, slot, tail):
            for n, u in enumerate(body_units):
                before = body_units[n - 1] if n else None
                after = body_units[n + 1] if n + 1 < len(body_units) else None
                for k in range(u.pairs):
                    slot(u, k, before, after)
            tail(body_units[-1])

        def step(u):
            return PAIRS // u.pairs

        def pair_no(u, k):
            return u.no * PAIRS + k * step(u)

        def query_source(u):
            return xlow[:, :] if u.kind == "low" else (xself if u.kind == "self" else xcross)[:, u.half, :]

        def key_source(u):
            return xpatch[:, u.half, :] if u.kind == "cross" else query_source(u)

        def which(u):
            return 1 if u.kind == "cross" else 0

        FINISH = {"self": {"project": 1, "spread": 2, "pool": 3},
                  "cross": {"project": 0, "spread": 1, "hidden": 2, "out": 3},
                  "low": {}}

        def at(before, stage, k):
            return before is not None and FINISH[before.kind].get(stage) == k

        block = ctx.enter_context(nc.Block())

        setup_loads = []
        for m in range(2):
            setup_loads += [(wq_sb[:, m, :], wq[m]), (wk_sb[:, m, :], wk[m]), (wv_sb[:, m, :], wv[m])]
            setup_loads += [(wf_sb[64 * h2:64 * h2 + 64, m, :], wf[m][h2]) for h2 in range(2)]
        setup_loads += [
            (w1_sb[:, :], w1), (w2_sb[:, :, :], w2.rearrange("(b f) n -> f b n", b=FB)), (b1_sb[:, :], b1),
            (gain[:, :], gains), (shift[:, :], shifts), (bn_sb[:, :], bn), (ident[:, :], consts[:, 0:128]),
            (headmask[:, :], consts[:, 128:132]), (half_neg[:, :], consts[:, 132:136]),
            (eps[:, :], consts[:, 264:268]),
            (ones2_f[:, :], consts[0:2, 136:264]), (brow_f[:, :], bias_rows),
            (hid[:, 0:3, :].rearrange("p a b -> p (a b)")[:, 0:TAPS * C], convw)]

        @block.sync
        def _(sp):
            for to, src in setup_loads:
                sp.dma_start(to, src).then_inc(s_setup, 16)
            sp.wait_ge(s_prep_v, 2)
            for r in range(PAIRS):
                for part, src in ((0, brow_hi), (1, brow_lo)):
                    sp.dma_start(brow[part:part + 1, :, r, :],
                                 src[:, :].rearrange("p (a c) -> p a c", a=3)).then_inc(s_brow, 16)

            def body(units, n, i):
                for u in units:
                    strip = bass.ds(u.body * 2 + u.half, 1)
                    sp.wait_ge(s_y, u.no - u.half if len(units) == 2 else u.no - 3)
                    if u.kind == "self":
                        sp.dma_start(xself[:, u.half, :], x[strip, :, :].rearrange("a c t -> (a c) t")
                                     ).then_inc(s_xself_in[u.half], 16)
                    else:
                        sp.wait_ge(s_self_stored[u.half], u.body * 16 + 16)
                        sp.dma_start(xcross[:, u.half, :], self_out[strip, :, :].rearrange("a c t -> (a c) t")
                                     ).then_inc(s_xcross[u.half], 16)

            walk(nc.sync.Fori, body, lambda low, image: None)

            for h in range(2):
                sp.wait_ge(s_x2_stored[h], 16 * IMAGES * PER)
            def chunk(dram, image, q):
                return dram[bass.ds(image, 1), :, q * CHUNK:(q + 1) * CHUNK].rearrange("a c t -> (a c) t")

            def load(image, q):
                sp.wait_ge(s_last_out[q], image * 16)
                sp.dma_start(lastx[:, q, :], chunk(ffn_out, image, q)).then_inc(s_last_in[q], 16)

            def store(image, q):
                sp.wait_ge(s_sum, image * CHUNKS + q + 1)
                sp.dma_start(chunk(out, image, q), lastx[:, q, :]).then_inc(s_last_out[q], 16)

            for q in range(CHUNKS):
                load(0, q)
            with nc.sync.Fori(0, IMAGES - 1) as i:
                for q in range(CHUNKS + 1):
                    if q < CHUNKS:
                        store(i, q)
                    if q:
                        load(i + 1, q - 1)
            for q in range(CHUNKS):
                store(IMAGES - 1, q)
            for q in range(CHUNKS):
                sp.wait_ge(s_last_out[q], 16 * IMAGES)

        @block.tensor
        def _(pe):
            mm = nc.tensor.matmul

            def project(u, kind):
                w = (wq_sb if kind == "q" else wk_sb)[:, which(u), :]
                src = (query_source(u) if kind == "q" else key_source(u)).rearrange(
                    "c (p w t) -> c p w t", w=2, t=TOK)
                n = u.pairs * TOK
                for g in range(2):
                    for win in range(2):
                        last = mm(ps_proj[64 * win:64 * win + 64, g * n:(g + 1) * n], w[:, 64 * g:64 * g + 64],
                                  src[:, :, win, :], start=True, stop=True, skip_group_check=True)
                last.then_inc(s_q if kind == "q" else s_k, 1)

            def project_q(u):
                if u.kind == "self":
                    pe.wait_ge(s_xself_in[u.half], u.body * 16 + 16)
                elif u.kind == "cross":
                    pe.wait_ge(s_xcross[u.half], u.body * 16 + 16)
                else:
                    pe.wait_ge(s_xlow, u.body + 1)
                pe.wait_ge(s_proj_free, u.no * 3)
                project(u, "q")

            def project_k(u):
                if u.kind == "cross":
                    pe.wait_ge(s_xpatch, u.body * 2 + u.half + 1)
                pe.wait_ge(s_proj_free, u.no * 3 + 1)
                project(u, "k")

            def project_v(u):
                pe.wait_ge(s_proj_free, u.no * 3 + 2)
                src = key_source(u)
                for p in range(u.pairs):
                    last = mm(ps_proj[:, C * p:C * p + C], src[:, C * p:C * p + C], wv_sb[:, which(u), :],
                              start=True, stop=True, skip_group_check=True)
                last.then_inc(s_v, 1)

            def rough_scores(u, k):
                if k == 0:
                    pe.wait_ge(s_qm, u.no + 1)
                    pe.wait_ge(s_khi, u.no + 1)
                for j in range(4):
                    a = (j // 2) * u.pairs + k
                    last = mm(ps_max[:, 128 * j:128 * j + 128],
                              qm_hi[:, u.par, a, 2 * (j % 2):2 * (j % 2) + 2, :].rearrange("p h t -> p (h t)"),
                              ks_hi[:, u.par, a, :, :].rearrange("p w t -> p (w t)"),
                              start=True, stop=True, skip_group_check=True)
                last.then_inc(s_max, step(u))

            def scores(u, k):
                ps = ps_s[k % 2]
                if k == 0:
                    pe.wait_ge(s_proj_free, u.no * 3 + 2)
                for g in range(2):
                    a = g * u.pairs + k
                    for n, (kk, qq) in enumerate(((ks_hi, qm_hi), (ks_hi, qm_lo), (ks_lo, qm_hi))):
                        mm(ps[:, 256 * g:256 * g + 256], kk[:, u.par, a, :, :].rearrange("p w t -> p (w t)"),
                           qq[:, u.par, a, :, :].rearrange("p h t -> p (h t)"),
                           start=(g == 0 and n == 0), stop=False, skip_group_check=True)
                pe.wait_ge(s_negb, pair_no(u, k) + step(u))
                for j in range(4):
                    last = mm(ps[:, 128 * j:128 * j + 128],
                              negmax_b[:, k % 2, 2 * j:2 * j + 2, :].rearrange("p w t -> p (w t)"),
                              identb[:, :], start=False, stop=True, skip_group_check=True)
                last.then_inc(s_s, step(u))

            def weigh(u, k):
                if k == 0:
                    pe.wait_ge(s_proj_free, u.no * 3 + 3)
                pe.wait_ge(s_prob, pair_no(u, k) + step(u))
                pe.wait_ge(s_on, pair_no(u, k))
                for j in range(4):
                    last = mm(ps_o[:, VC * j:VC * j + VC], prob[:, k % 2, 128 * j:128 * j + 128],
                              vb[:, u.par, 4 * k + j, :], start=True, stop=True, skip_group_check=True)
                last.then_inc(s_pv, step(u))

            def turn_heads(u):
                pe.wait_ge(s_on, u.no * PAIRS + PAIRS)
                pe.wait_ge(s_xt_out, u.no)
                pe.wait_ge(s_sign, u.crosses)
                for p in range(u.pairs):
                    last = mm(ps_t[:, C * p:C * p + C], onorm[:, u.par, p, :], ident[:, :], is_transpose=True,
                              start=True, stop=True, skip_group_check=True)
                last.then_inc(s_ot, 1)
                residual(u, query_source(u), which(u))

            def residual(u, src, bias):
                for p in range(u.pairs):
                    mm(ps_y[:, C * p:C * p + C], src[:, C * p:C * p + C], ident[:, :], is_transpose=True,
                       start=(p == 0), stop=False, skip_group_check=True)
                mm(ps_y[:, 0:C * u.pairs], ones2[:, :],
                   brow[:, bias, 0:u.pairs, :].rearrange("p a c -> p (a c)"), start=False, stop=False,
                   skip_group_check=True)

            def project_out(u):
                pe.wait_ge(s_oT, u.no + 1)
                for p in range(u.pairs):
                    last = mm(ps_y[:, C * p:C * p + C], oT[:, C * p:C * p + C], wf_sb[:, which(u), :],
                              start=False, stop=True, skip_group_check=True)
                last.then_inc(s_y, 1)

            def turn_tokens(pairs, done):
                for p in range(pairs):
                    last = mm(ps_t[:, C * p:C * p + C], xn[:, C * p:C * p + C], ident[:, :], is_transpose=True,
                              start=True, stop=True, skip_group_check=True)
                last.then_inc(done, 1)

            def spread(u):
                pe.wait_ge(s_xn, u.no + 1)
                turn_tokens(u.pairs, s_xt)

            def hidden(u, image):
                pe.wait_ge(s_xt_out, u.no + 1)
                for b in range(FB + 1):
                    if b < FB:
                        pe.wait_ge(s_relu, u.crosses * FB + b)
                        if b == 0:
                            pe.wait_ge(s_yconv, image * STRIPS)
                        mm(ps_hid[:, :], w1_sb[:, C * b:C * b + C], xf[:, :], start=True, stop=True,
                           skip_group_check=True).then_inc(s_hid, 1)
                    if b == 0:
                        residual(u, xf, 2)
                        continue
                    if b == FB:
                        pe.wait_ge(s_relu, u.crosses * FB + FB)
                    for p in range(PAIRS):
                        last = mm(ps_y[:, C * p:C * p + C], hid[:, b - 1, C * p:C * p + C], w2_sb[:, b - 1, :],
                                  start=False, stop=(b == FB), skip_group_check=True)
                last.then_inc(s_y2, 1)

            def turn_out(u):
                pe.wait_ge(s_xn2, u.crosses + 1)
                turn_tokens(PAIRS, s_xt2)

            def conv(image, s):
                if s == 0:
                    pe.wait_ge(s_sign, image * STRIPS + STRIPS)
                    pe.wait_ge(s_relu, image * STRIPS * FB + STRIPS * FB)
                else:
                    pe.wait_ge(s_yconv, image * STRIPS + s)
                for t in range(TAPS):
                    dy, dx = t // 3, t % 3
                    last = mm(ps_hid[:, :].rearrange("p (r w) -> p r w", r=WIN), convs[:, t, :],
                              smap[:, WIN * s + dy:WIN * s + dy + WIN, dx:dx + W],
                              start=(t == 0), stop=(t == TAPS - 1), skip_group_check=True)
                last.then_inc(s_conv, 1)

            pe.wait_ge(s_setup, 16 * len(setup_loads))
            pe.wait_ge(s_brow, 16 * 2 * PAIRS)
            pe.wait_ge(s_prep_v, 3)
            pe.wait_ge(s_prep_a, 1)
            pe.wait_ge(s_prep_g, 2)

            def head(u):
                project_q(u)
                project_k(u)
                project_v(u)
                rough_scores(u, 0)
                scores(u, 0)

            def body(units, n, i):
                def slot(u, k, before, after):
                    nxt = (u, k + 1) if k + 1 < u.pairs else ((after, 0) if after else None)
                    if nxt:
                        rough_scores(*nxt)
                    if at(before, "project", k):
                        turn_heads(before)
                    if after and k < 3:
                        (project_q, project_k, project_v)[k](after)
                    if nxt:
                        scores(*nxt)
                    if at(before, "project", k):
                        project_out(before)
                    if at(before, "spread", k):
                        spread(before)
                    if at(before, "hidden", k):
                        hidden(before, n)
                    if at(before, "out", k):
                        turn_out(before)
                    weigh(u, k)

                def tail(u):
                    turn_heads(u)
                    project_out(u)
                    spread(u)
                    if u.kind == "cross":
                        hidden(u, n)
                        turn_out(u)

                head(units[0])
                slots(units, slot, tail)

            def section(low, image):
                filler = iter(range(STRIPS if image is not None else 0))

                def some_conv(count):
                    for _ in range(count):
                        s = next(filler, None)
                        if s is not None:
                            conv(image, s)

                if low:
                    head(low)
                    some_conv(1)
                    rough_scores(low, 1)
                    scores(low, 1)
                    weigh(low, 0)
                    some_conv(1)
                    weigh(low, 1)
                    some_conv(1)
                    turn_heads(low)
                    some_conv(1)
                    project_out(low)
                    some_conv(2)
                    spread(low)
                some_conv(STRIPS)

            walk(nc.tensor.Fori, body, section)

        @block.scalar
        def _(act):
            activation = nc.scalar.activation

            def take_q(u):
                act.wait_ge(s_q, u.no + 1)
                n = 2 * u.pairs * TOK
                activation(qc_hi[:, 0:n], ps_proj[:, 0:n], ACT.Identity, scale=QS).then_inc(s_qhi, 1)

            def take_k(u):
                act.wait_ge(s_k, u.no + 1)
                a = 2 * u.pairs
                for win in range(2):
                    r = slice(64 * win, 64 * win + 64)
                    last = activation(ks_hi[r, u.par, 0:a, win, :],
                                      ps_proj[r, 0:a * TOK].rearrange("p (a t) -> p a t", a=a), ACT.Identity)
                last.then_inc(s_khi, 1)

            def take_v(u):
                act.wait_ge(s_v, u.no + 1)
                a = 4 * u.pairs
                for win in range(2):
                    r = slice(64 * win, 64 * win + 64)
                    last = activation(vb[r, u.par, 0:a, 32 * win:32 * win + 32],
                                      ps_proj[r, 0:a * 32].rearrange("p (a t) -> p a t", a=a), ACT.Identity)
                last.then_inc(s_proj_free, 1)

            def exponentials(u, k):
                act.wait_ge(s_s, pair_no(u, k) + step(u))
                activation(prob[:, k % 2, :], ps_s[k % 2][:, :], ACT.Exp).then_inc(s_prob, step(u))

            def take_turned(u):
                act.wait_ge(s_ot, u.no + 1)
                n = u.pairs * C
                src = ps_t[:, 0:n].rearrange("p (a h t) -> p a h t", h=2, t=TOK)
                to = oT[:, 0:n].rearrange("p (a w t) -> p a w t", w=2, t=TOK)
                for win in range(2):
                    for h2 in range(2):
                        last = activation(to[64 * h2:64 * h2 + 64, :, win, :], src[64 * win:64 * win + 64, :, h2, :],
                                          ACT.Identity)
                last.then_inc(s_oT, 1)

            def take_output(u):
                act.wait_ge(s_xt, u.no + 1)
                if u.kind == "self":
                    act.wait_ge(s_self_stored[u.half], u.body * 16)
                    act.wait_ge(s_colsum, u.body * 2 + u.half)
                    to = xa[:, u.half, :]
                elif u.kind == "cross":
                    to = xf[:, :]
                else:
                    act.wait_ge(s_kv0, u.body)
                    to = low_out[:, :]
                m = which(u)
                activation(to, ps_t[:, 0:u.pairs * C], ACT.Identity, bias=shift[:, m:m + 1],
                           scale=gain[:, m:m + 1]).then_inc(s_xt_out, 1)

            def store_self(u):
                act.wait_ge(s_xt_out, u.no + 1)
                act.dma_start(self_out[bass.ds(u.body * 2 + u.half, 1), :, :].rearrange("a c t -> (a c) t"),
                              xa[:, u.half, :]).then_inc(s_self_stored[u.half], 16)

            def take_hidden(u):
                for b in range(FB):
                    act.wait_ge(s_hid, u.crosses * FB + b + 1)
                    activation(hid[:, b, :], ps_hid[:, :], ACT.Relu, bias=b1_sb[:, b:b + 1]).then_inc(s_relu, 1)

            def take_out(u, image, i):
                act.wait_ge(s_xt2, u.crosses + 1)
                act.wait_ge(s_x2_stored[u.half], u.body * 16)
                src = ps_t[:, :].rearrange("p (v r w) -> p v r w", v=WIN, r=WIN)
                activation(x2[:, u.half, :].rearrange("p (r v w) -> p v r w", r=WIN, v=WIN), src, ACT.Identity,
                           bias=shift[:, 2:3], scale=gain[:, 2:3]).then_inc(s_x2, 1)
                act.wait_ge(s_conv, image * STRIPS)
                rows = smap[:, bass.ds(i * 2 * WIN + (u.half * WIN + 1), WIN), 1:1 + W]
                activation(rows.rearrange("p r (v w) -> p v r w", v=WIN), src, ACT.Sign,
                           bias=shift[:, 2:3], scale=gain[:, 2:3]).then_inc(s_sign, 1)
                act.wait_ge(s_x2, u.crosses + 1)
                act.dma_start(ffn_out[bass.ds(image, 1), :, bass.ds(i * 2 * SW + u.half * SW, SW)
                                      ].rearrange("a c t -> (a c) t"),
                              x2[:, u.half, :]).then_inc(s_x2_stored[u.half], 16)

            def take_conv(image, s):
                act.wait_ge(s_conv, image * STRIPS + s + 1)
                activation(yconv[:, bass.ds(image * H * W + s * SW, SW)], ps_hid[:, :], ACT.Identity
                           ).then_inc(s_yconv, 1)

            act.wait_ge(s_setup, 16 * len(setup_loads))
            activation(convs[:, :, :].rearrange("p a b -> p (a b)"),
                       hid[:, 0:3, :].rearrange("p a b -> p (a b)")[:, 0:TAPS * C], ACT.Sign).then_inc(s_prep_a, 1)
            act.wait_ge(s_prep_v, 3)
            act.wait_ge(s_prep_g, 2)
            act.wait_ge(s_prep_a, 1)

            def head(u):
                take_q(u)
                take_k(u)
                take_v(u)
                exponentials(u, 0)

            def body(units, n, i):
                def slot(u, k, before, after):
                    nxt = (u, k + 1) if k + 1 < u.pairs else ((after, 0) if after else None)
                    if at(before, "project", k):
                        take_turned(before)
                    if after and k < 3:
                        (take_q, take_k, take_v)[k](after)
                    if nxt:
                        exponentials(*nxt)
                    if at(before, "spread", k):
                        take_output(before)
                    if at(before, "hidden", k):
                        take_hidden(before)
                    if at(before, "pool", k):
                        store_self(before)
                    if at(before, "out", k):
                        take_out(before, n, i)

                def tail(u):
                    take_turned(u)
                    take_output(u)
                    if u.kind == "cross":
                        take_hidden(u)
                        take_out(u, n, i)
                    else:
                        store_self(u)

                head(units[0])
                slots(units, slot, tail)

            def section(low, image):
                filler = iter(range(STRIPS if image is not None else 0))

                def some_conv(count):
                    for _ in range(count):
                        s = next(filler, None)
                        if s is not None:
                            take_conv(image, s)

                if low:
                    head(low)
                    some_conv(1)
                    exponentials(low, 1)
                    some_conv(2)
                    take_turned(low)
                    some_conv(3)
                    take_output(low)
                some_conv(STRIPS)

            walk(nc.scalar.Fori, body, section)

            act.wait_ge(s_bnab, 3)
            with nc.scalar.Fori(0, IMAGES) as i:
                for q in range(CHUNKS):
                    act.wait_ge(s_sum, i * CHUNKS + (q - 1) if q else i * CHUNKS)
                    activation(lasty[:, q % 2, :], yconv[:, bass.ds(i * H * W + q * CHUNK, CHUNK)], ACT.Identity,
                               bias=bnv[:, 6:7], scale=bnv[:, 4:5]).then_inc(s_affine, 1)

        @block.vector
        def _(dve):
            v = nc.vector

            def split_q(u):
                dve.wait_ge(s_qhi, u.no + 1)
                a = 2 * u.pairs
                v.scalar_tensor_tensor(out=qc_lo[:, 0:a * TOK], in0=ps_proj[:, 0:a * TOK], scalar=QS,
                                       in1=qc_hi[:, 0:a * TOK], op0=ALU.mult, op1=ALU.subtract
                                       ).then_inc(s_proj_free, 1)
                dve.wait_ge(s_proj_free, u.no * 3 + 1)
                for src, to in ((qc_hi, qm_hi), (qc_lo, qm_lo)):
                    for h in range(4):
                        last = v.tensor_scalar(to[:, u.par, 0:a, h, :],
                                               src[:, 0:a * TOK].rearrange("p (a t) -> p a t", a=a),
                                               headmask[:, h:h + 1], None, ALU.mult)
                last.then_inc(s_qm, 1)

            def split_k(u):
                dve.wait_ge(s_khi, u.no + 1)
                a = 2 * u.pairs
                for win in range(2):
                    r = slice(64 * win, 64 * win + 64)
                    last = v.tensor_tensor(ks_lo[r, u.par, 0:a, win, :],
                                           ps_proj[r, 0:a * TOK].rearrange("p (a t) -> p a t", a=a),
                                           ks_hi[r, u.par, 0:a, win, :], ALU.subtract)
                last.then_inc(s_proj_free, 1)

            def maxima(u, k):
                dve.wait_ge(s_max, pair_no(u, k) + step(u))
                v.tensor_reduce(negmax[:, k % 2, :], ps_max[:, :].rearrange("p (a t) -> p a t", t=TOK), AX.X,
                                ALU.max, negate=True).then_inc(s_neg, step(u))
                dve.wait_ge(s_neg, pair_no(u, k) + step(u))
                v.tensor_copy(negmax_b[:, k % 2, :, :],
                              negmax[:, k % 2, :].unsqueeze(2).to_broadcast([128, 8, TOK])
                              ).then_inc(s_negb, step(u))

            def normalise(u, k):
                dve.wait_ge(s_pv, pair_no(u, k) + step(u))
                blocks = ps_o[:, 0:4 * VC].rearrange("p (j c) -> p j c", j=4)
                v.reciprocal(rden[:, k % 2, :, :], blocks[:, :, 64:66]).then_inc(s_rden, step(u))
                dve.wait_ge(s_rden, pair_no(u, k) + step(u))
                for h2 in range(2):
                    r = slice(64 * h2, 64 * h2 + 64)
                    last = v.tensor_tensor(
                        onorm[r, u.par, k, :].rearrange("p (w j d) -> p j w d", w=2, j=4),
                        blocks[r, :, 0:64].rearrange("p j (w h d) -> p j w h d", w=2, h=2)[:, :, :, h2, :],
                        rden[r, k % 2, :, :].unsqueeze(3).to_broadcast([64, 4, 2, DH]), ALU.mult)
                last.then_inc(s_on, step(u))

            def norm_stats(pairs, count, done, stats_done, mv_done):
                dve.wait_ge(done, count)
                for p in range(pairs):
                    last = v.bn_stats(stats[:, p, :], ps_y[:, C * p:C * p + C])
                last.then_inc(stats_done, 1)
                dve.wait_ge(stats_done, count)
                dve.sem_inc(s_aggr, 1)
                for p in range(pairs):
                    last = v.bn_aggr(mv[:, p, :], stats[:, p, :])
                last.then_inc(mv_done, 1)

            def norm_apply(pairs, count, rstd_done, done):
                dve.wait_ge(rstd_done, count)
                for p in range(pairs):
                    last = v.tensor_scalar(xn[:, C * p:C * p + C], ps_y[:, C * p:C * p + C], mv[:, p, 0:1],
                                           rstd[:, p:p + 1], ALU.subtract, ALU.mult)
                last.then_inc(done, 1)

            def stats1(u):
                norm_stats(u.pairs, u.no + 1, s_y, s_stats, s_mv)

            def apply1(u):
                norm_apply(u.pairs, u.no + 1, s_rstd, s_xn)

            def stats2(u):
                norm_stats(PAIRS, u.crosses + 1, s_y2, s_stats2, s_mv2)

            def apply2(u):
                norm_apply(PAIRS, u.crosses + 1, s_rstd2, s_xn2)

            def pool(u, i):
                strip = u.body * 2 + u.half
                dve.wait_ge(s_xt_out, u.no + 1)
                dve.wait_ge(s_pooled, strip)
                v.tensor_reduce(colsum[:, :], xa[:, u.half, :].rearrange("p (a f) -> p a f", f=DOWN), AX.X,
                                ALU.add).then_inc(s_colsum, 1)
                dve.wait_ge(s_colsum, strip + 1)
                v.tensor_reduce(low_sum[:, bass.ds(i * 2 + u.half, 1), :].rearrange("p a (w c) -> p (a w) c", c=2),
                                colsum[:, :].rearrange("p (w r c) -> p w c r", r=DOWN, c=2), AX.X,
                                ALU.add).then_inc(s_pooled, 1)

            def make_low(low):
                dve.wait_ge(s_pooled, low.body * STRIPS + STRIPS)
                q = LH // WIN
                for wi in range(q):
                    last = v.tensor_scalar(
                        xlow[:, :].rearrange("p (a b s t) -> p a b s t", a=q, b=q, s=4)[:, wi, :, :, :],
                        low_sum[:, 4 * wi:4 * wi + 4, :].rearrange("p s (b t) -> p b s t", b=q),
                        1.0 / (DOWN * DOWN), None, ALU.mult)
                last.then_inc(s_xlow, 1)

            def pad_low(low):
                dve.wait_ge(s_xt_out, low.no + 1)
                dve.wait_ge(s_xpatch, low.body * STRIPS)
                q = LH // WIN
                for wi in range(q):
                    for wj in range(q):
                        src = low_out[:, :].rearrange("p (a s v r c) -> p a s v r c", a=q * q, s=4, v=4, r=2)
                        for r in range(2):
                            rows = kvpad[:, WIN * wi:WIN * wi + WIN, WIN * wj:WIN * wj + WIN]
                            last = v.tensor_copy(
                                rows.rearrange("p (s r) (v c) -> p s r v c", r=2, c=2)[:, :, r, :, :],
                                src[:, q * wi + wj, :, :, r, :])
                last.then_inc(s_kv0, 1)
                dve.wait_ge(s_kv0, low.body + 1)
                v.tensor_copy(kvpad[:, 0:LH, LH:KP], kvpad[:, 0:LH, 0:KP - LH]).then_inc(s_kv1, 1)
                dve.wait_ge(s_kv1, low.body + 1)
                v.tensor_copy(kvpad[:, LH:KP, :], kvpad[:, 0:KP - LH, :]).then_inc(s_kv, 1)

            def conv_stats(image, s):
                dve.wait_ge(s_yconv, image * STRIPS + s + 1)
                v.bn_stats(ystats[:, bass.ds(image * STRIPS + s, 1), :].rearrange("p a b -> p (a b)"),
                           yconv[:, bass.ds(image * H * W + s * SW, SW)]).then_inc(s_ystats, 1)

            dve.wait_ge(s_setup, 16 * len(setup_loads))
            v.tensor_copy(brow_hi[:, :], brow_f[:, :]).then_inc(s_prep_v, 1)
            dve.wait_ge(s_prep_v, 1)
            v.tensor_tensor(brow_lo[:, :], brow_f[:, :], brow_hi[:, :], ALU.subtract).then_inc(s_prep_v, 1)
            v.tensor_copy(ones2[:, :], ones2_f[:, :])
            v.tensor_copy(identb[:, :], ident[:, :])
            v.memset(ks_hi[:, :, :, :, :], 0.0)
            v.memset(ks_lo[:, :, :, :, :], 0.0).then_inc(s_prep_v, 1)
            dve.wait_ge(s_prep_v, 3)
            dve.wait_ge(s_prep_g, 2)

            def head(u):
                split_q(u)
                split_k(u)
                maxima(u, 0)

            def body(units, n, i):
                def slot(u, k, before, after):
                    nxt = (u, k + 1) if k + 1 < u.pairs else ((after, 0) if after else None)
                    if at(before, "spread", k):
                        apply1(before)
                    if at(before, "out", k):
                        apply2(before)
                    if nxt:
                        maxima(*nxt)
                    if after and k < 2:
                        (split_q, split_k)[k](after)
                    if at(before, "pool", k):
                        pool(before, i)
                    if at(before, "project", k):
                        stats1(before)
                    if at(before, "hidden", k):
                        stats2(before)
                    normalise(u, k)

                def tail(u):
                    stats1(u)
                    apply1(u)
                    if u.kind == "cross":
                        stats2(u)
                        apply2(u)
                    else:
                        pool(u, i)

                head(units[0])
                slots(units, slot, tail)

            def section(low, image):
                if low:
                    make_low(low)
                    head(low)
                    maxima(low, 1)
                    normalise(low, 0)
                    normalise(low, 1)
                    stats1(low)
                    apply1(low)
                    pad_low(low)
                if image is not None:
                    for s in range(STRIPS):
                        conv_stats(image, s)

            walk(nc.vector.Fori, body, section)

            dve.wait_ge(s_ystats, IMAGES * STRIPS)
            v.bn_aggr(bnv[:, 0:2], ystats[:, :, :].rearrange("p a b -> p (a b)")).then_inc(s_bn, 1)
            dve.wait_ge(s_bnr, 2)
            v.tensor_tensor(bnv[:, 4:5], bnv[:, 3:4], bn_sb[:, 0:1], ALU.mult).then_inc(s_bnab, 1)
            dve.wait_ge(s_bnab, 1)
            v.tensor_tensor(bnv[:, 5:6], bnv[:, 0:1], bnv[:, 4:5], ALU.mult).then_inc(s_bnab, 1)
            dve.wait_ge(s_bnab, 2)
            v.tensor_tensor(bnv[:, 6:7], bn_sb[:, 1:2], bnv[:, 5:6], ALU.subtract).then_inc(s_bnab, 1)
            with nc.vector.Fori(0, IMAGES) as i:
                for q in range(CHUNKS):
                    dve.wait_ge(s_last_in[q], i * 16 + 16)
                    dve.wait_ge(s_affine, i * CHUNKS + q + 1)
                    v.tensor_tensor(lastx[:, q, :], lastx[:, q, :], lasty[:, q % 2, :], ALU.add).then_inc(s_sum, 1)

        @block.gpsimd
        def _(pool):
            g = nc.gpsimd

            def inv_sqrt(pairs, count, mv_done, var_done, rstd_done):
                pool.wait_ge(mv_done, count)
                g.tensor_tensor(vareps[:, 0:pairs], mv[:, 0:pairs, 1], eps[:, 0:pairs], ALU.add).then_inc(var_done, 1)
                pool.wait_ge(var_done, count)
                g.tensor_tensor(rstd[:, 0:pairs], vareps[:, 0:pairs], half_neg[:, 0:pairs], ALU.pow
                                ).then_inc(rstd_done, 1)

            def rstd1(u):
                inv_sqrt(u.pairs, u.no + 1, s_mv, s_var, s_rstd)

            def rstd2(u):
                inv_sqrt(PAIRS, u.crosses + 1, s_mv2, s_var2, s_rstd2)

            def gather(u, units, n, i):
                pool.wait_ge(s_kv, n + 1)
                pool.wait_ge(s_y, u.no - u.half if len(units) == 2 else u.no - 3)
                rows = kvpad[:, bass.ds(i * 2 * STRIDE + u.half * STRIDE, WIN), :]
                for win in range(STRIPS):
                    last = g.tensor_copy(
                        xpatch[:, u.half, TOK * win:TOK * win + TOK].rearrange("p (r c) -> p r c", r=WIN),
                        rows[:, :, STRIDE * win:STRIDE * win + WIN])
                last.then_inc(s_xpatch, 1)

            pool.wait_ge(s_setup, 16 * len(setup_loads))
            g.memset(smap[:, :, :], 0.0)
            g.memset(vb[:, :, :, :], 0.0).then_inc(s_prep_g, 1)
            pool.wait_ge(s_prep_g, 1)
            for win in range(2):
                last = g.memset(vb[64 * win:64 * win + 64, :, :, 64 + win:65 + win], 1.0)
            last.then_inc(s_prep_g, 1)

            def body(units, n, i):
                for u in units:
                    if u.kind == "cross":
                        gather(u, units, n, i)

                def slot(u, k, before, after):
                    if at(before, "project", k):
                        rstd1(before)
                    if at(before, "hidden", k):
                        rstd2(before)

                def tail(u):
                    rstd1(u)
                    if u.kind == "cross":
                        rstd2(u)

                slots(units, slot, tail)

            walk(nc.gpsimd.Fori, body, lambda low, image: rstd1(low) if low else None)
            pool.wait_ge(s_bn, 1)
            g.tensor_tensor(bnv[:, 2:3], bnv[:, 1:2], eps[:, 0:1], ALU.add).then_inc(s_bnr, 1)
            pool.wait_ge(s_bnr, 1)
            g.tensor_tensor(bnv[:, 3:4], bnv[:, 2:3], half_neg[:, 0:1], ALU.pow).then_inc(s_bnr, 1)


def kernel(**inputs):
    import numpy as np
    import concourse.bacc as bacc
    from concourse.bass_utils import run_bass_kernel_spmd

    a = {k: np.asarray(t) for k, t in inputs.items()}
    L0 = {k[len("L0_conv_"):]: t for k, t in a.items() if k.startswith("L0_conv_")}
    both = lambda name: np.stack([L0["sa_" + name], L0["ca_" + name]])
    consts = np.zeros((128, 268), np.float32)
    consts[:, 0:128] = np.eye(128)
    for h in range(4):
        for win in range(2):
            consts[win * 64 + h * DH:win * 64 + h * DH + DH, 128 + h] = 1.0
    consts[:, 132:136] = -0.5
    consts[:, 136:264] = 1.0
    consts[:, 264:268] = EPS
    arrays = {
        "x": a["x"].reshape(IMAGES, C, STRIPS, WIN, W // WIN, WIN).transpose(0, 2, 1, 4, 3, 5
                                                                             ).reshape(IMAGES * STRIPS, C, SW),
        "wq": both("wq"), "wk": both("wk"), "wv": both("wv"),
        "wf": both("wf").reshape(2, HEADS // 2, 2, DH, C).transpose(0, 2, 1, 3, 4).reshape(2, 2, C // 2, C),
        "bias_rows": np.stack([L0["sa_bf"], L0["ca_bf"], L0["ffn_b2"]]).reshape(1, 3 * C),
        "gains": np.stack([L0["ln_self_g"], L0["ln_cross_g"], L0["ln_out_g"]], axis=1),
        "shifts": np.stack([L0["ln_self_b"], L0["ln_cross_b"], L0["ln_out_b"]], axis=1),
        "b1": L0["ffn_b1"].reshape(FB, C).T,
        "w1": L0["ffn_w1"], "w2": L0["ffn_w2"],
        "convw": a["L1_conv_weight"].transpose(1, 2, 3, 0).reshape(C, TAPS * C),
        "bn": np.stack([a["L1_conv_gamma"], a["L1_conv_beta"]], axis=1),
        "consts": consts,
    }
    nc = bacc.Bacc("TRN2", target_bir_lowering=False, num_devices=1)
    maps, args = {}, {}
    for name, t in arrays.items():
        t = np.ascontiguousarray(t)
        maps["in_" + name] = t
        args[name] = nc.dram_tensor("in_" + name, t.shape, F32, kind="ExternalInput").ap()
    out = nc.dram_tensor("out_0", (IMAGES, C, H * W), F32, kind="ExternalOutput").ap()
    attention_conv(nc, out=out, **args)
    r = run_bass_kernel_spmd(nc, [maps], core_ids=[0])
    return r.results[0]["out_0"].reshape(IMAGES, C, H, W)
```

```python
from contextlib import ExitStack
from collections import namedtuple

import concourse.bass as bass
from concourse import mybir

ALU = mybir.AluOpType
ACT = mybir.ActivationFunctionType
AX = mybir.AxisListType
F32 = mybir.dt.float32
F16 = mybir.dt.float16
BF16 = mybir.dt.bfloat16

IMAGES, C, H, W = 8, 128, 64, 64
WIN = 8
TOK = WIN * WIN
HEADS = 8
DH = C // HEADS
STRIPS = H // WIN
SW = WIN * W
PAIRS = SW // (2 * TOK)
DOWN = 4
LH = H // DOWN
LT = LH * LH
LPAIRS = LT // (2 * TOK)
STRIDE = WIN // DOWN
KP = LH - STRIDE + WIN
DF = 512
FB = DF // C
VC = 96
MAP = W + 2
TAPS = 9
EPS = 1e-5
QS = DH ** -0.5
CHUNK = 1024
CHUNKS = H * W // CHUNK
PER = STRIPS // 2

Unit = namedtuple("Unit", "kind half par no pairs body crosses image i")


def attention_conv(nc, x, wq, wk, wv, wf, bias_rows, gains, shifts, b1, w1, w2, convw, bn, consts, out):
    with ExitStack() as ctx:
        def sb(name, shape, dt=F32):
            return ctx.enter_context(nc.sbuf_tensor(name, shape, dt))

        def bank(name):
            return ctx.enter_context(nc.psum_tensor(name, [128, 512], F32))

        def sem(name):
            return ctx.enter_context(nc.semaphore(name))

        self_out = nc.dram_tensor("self_out", (IMAGES * STRIPS, C, SW), F32, kind="Internal").ap()
        ffn_out = nc.dram_tensor("ffn_out", (IMAGES, C, H * W), F32, kind="Internal").ap()

        wq_sb, wk_sb, wv_sb, wf_sb = (sb(n, [128, 2, C]) for n in ("wq_sb", "wk_sb", "wv_sb", "wf_sb"))
        w1_sb = sb("w1_sb", [128, DF])
        w2_sb = sb("w2_sb", [128, FB, C])
        b1_sb = sb("b1_sb", [128, FB])
        gain = sb("gain", [128, 3])
        shift = sb("shift", [128, 3])
        bn_sb = sb("bn_sb", [128, 2])
        convs = sb("convs", [128, TAPS, C], BF16)
        ident = sb("ident", [128, 128])
        headmask = sb("headmask", [128, 4])
        identb = sb("identb", [128, 128], BF16)
        ones2_f = sb("ones2_f", [2, 128])
        ones2 = sb("ones2", [2, 128], F16)
        brow_f = sb("brow_f", [1, 3 * C])
        brow_hi = sb("brow_hi", [1, 3 * C], F16)
        brow_lo = sb("brow_lo", [1, 3 * C], F16)
        brow = sb("brow", [2, 3, PAIRS, C], F16)
        half_neg = sb("half_neg", [128, PAIRS])
        eps = sb("eps", [128, PAIRS])

        xself = sb("xself", [128, 2, SW])
        xcross = sb("xcross", [128, 2, SW])
        xpatch = sb("xpatch", [128, 2, SW])
        xlow = sb("xlow", [128, LT])
        qc_hi = sb("qc_hi", [128, 8 * TOK], F16)
        qc_lo = sb("qc_lo", [128, 8 * TOK], F16)
        qm_hi = sb("qm_hi", [128, 2, 8, 4, TOK], F16)
        qm_lo = sb("qm_lo", [128, 2, 8, 4, TOK], F16)
        ks_hi = sb("ks_hi", [128, 2, 8, 2, TOK], F16)
        ks_lo = sb("ks_lo", [128, 2, 8, 2, TOK], F16)
        vb = sb("vb", [128, 2, PAIRS * 4, VC])
        negmax = sb("negmax", [128, 2, 8], BF16)
        negmax_b = sb("negmax_b", [128, 2, 8, TOK], BF16)
        prob = sb("prob", [128, 2, 512])
        rden = sb("rden", [128, 2, 4, 2])
        onorm = sb("onorm", [128, 2, PAIRS, C])
        oT = sb("oT", [128, SW])
        stats = sb("stats", [128, PAIRS, 6])
        mv = sb("mv", [128, PAIRS, 2])
        vareps = sb("vareps", [128, PAIRS])
        rstd = sb("rstd", [128, PAIRS])
        xn = sb("xn", [128, SW])
        stats2 = sb("stats2", [128, PAIRS, 6])
        mv2 = sb("mv2", [128, PAIRS, 2])
        vareps2 = sb("vareps2", [128, PAIRS])
        rstd2 = sb("rstd2", [128, PAIRS])
        xn2 = sb("xn2", [128, SW])
        xa = sb("xa", [128, 2, SW])
        colsum = sb("colsum", [128, SW // DOWN])
        low_sum = sb("low_sum", [128, STRIPS, 32])
        low_out = sb("low_out", [128, LT])
        kvpad = sb("kvpad", [128, KP, KP])
        xf = sb("xf", [128, SW])
        hid = sb("hid", [128, FB, SW])
        x2 = sb("x2", [128, 2, SW])
        smap = sb("smap", [128, MAP, MAP], BF16)
        yconv = sb("yconv", [128, IMAGES * H * W], F16)
        ystats = sb("ystats", [128, IMAGES * STRIPS, 6])
        bnv = sb("bnv", [128, 8])
        lastx = sb("lastx", [128, CHUNKS, CHUNK])
        lasty = sb("lasty", [128, 2, CHUNK])

        ps_proj, ps_hid, ps_max, ps_s, ps_o, ps_t, ps_y, ps_y2 = (
            bank(n) for n in ("ps_proj", "ps_hid", "ps_max", "ps_s", "ps_o", "ps_t", "ps_y", "ps_y2"))

        s_setup = sem("s_setup")
        s_brow = sem("s_brow")
        s_xself_in = [sem("s_xself_in0"), sem("s_xself_in1")]
        s_xcross = [sem("s_xcross0"), sem("s_xcross1")]
        s_self_stored = [sem("s_self_stored0"), sem("s_self_stored1")]
        s_x2_stored = [sem("s_x2_stored0"), sem("s_x2_stored1")]
        s_last_in = [sem(f"s_last_in{q}") for q in range(CHUNKS)]
        s_last_out = [sem(f"s_last_out{q}") for q in range(CHUNKS)]
        s_prep_v = sem("s_prep_v")
        s_prep_a = sem("s_prep_a")
        s_prep_g = sem("s_prep_g")
        s_xpatch = sem("s_xpatch")
        s_rstd = sem("s_rstd")
        s_rstd2 = sem("s_rstd2")
        s_q = sem("s_q")
        s_k = sem("s_k")
        s_v = sem("s_v")
        s_proj_free = sem("s_proj_free")
        s_qhi = sem("s_qhi")
        s_qm_hi = sem("s_qm_hi")
        s_qm_lo = sem("s_qm_lo")
        s_khi = sem("s_khi")
        s_ot = sem("s_ot")
        s_oT = sem("s_oT")
        s_resid = sem("s_resid")
        s_y = sem("s_y")
        s_stats = sem("s_stats")
        s_mv = sem("s_mv")
        s_var = sem("s_var")
        s_aggr = sem("s_aggr")
        s_gather = sem("s_gather")
        s_xn = sem("s_xn")
        s_xt = sem("s_xt")
        s_xt_out = sem("s_xt_out")
        s_max = sem("s_max")
        s_neg = sem("s_neg")
        s_negb = sem("s_negb")
        s_s = sem("s_s")
        s_prob = sem("s_prob")
        s_pv = sem("s_pv")
        s_rden = sem("s_rden")
        s_on = sem("s_on")
        s_hid = sem("s_hid")
        s_relu = sem("s_relu")
        s_y2 = sem("s_y2")
        s_stats2 = sem("s_stats2")
        s_mv2 = sem("s_mv2")
        s_var2 = sem("s_var2")
        s_xn2 = sem("s_xn2")
        s_xt2 = sem("s_xt2")
        s_x2 = sem("s_x2")
        s_sign = sem("s_sign")
        s_colsum = sem("s_colsum")
        s_pooled = sem("s_pooled")
        s_xlow = sem("s_xlow")
        s_kv0 = sem("s_kv0")
        s_kv1 = sem("s_kv1")
        s_kv = sem("s_kv")
        s_conv = sem("s_conv")
        s_yconv = sem("s_yconv")
        s_ystats = sem("s_ystats")
        s_bn = sem("s_bn")
        s_bnr = sem("s_bnr")
        s_bnab = sem("s_bnab")
        s_affine = sem("s_affine")
        s_sum = sem("s_sum")

        def pair_at(units, n):
            for u in units:
                if u is None or n < u.pairs:
                    return None if u is None else (u, n)
                n -= u.pairs

        def head(do, u, low):
            if low is not None and u.kind == "cross":
                do("apply", low)
                do("spread", low)
                do("pad_low", low)
                low = None
            do("gather", u)
            do("queries", u)
            if low is not None:
                do("apply", low)
            do("masks_hi", u)
            do("keys", u)
            if low is not None:
                do("spread", low)
            do("masks_lo", u)
            do("values", u)
            do("take_values", u)
            if low is not None:
                do("pad_low", low)
            do("rough", u, 0)
            do("scores", u, 0)
            do("rough", u, 1)

        ends_mixed = {
            "cross": ({0: ((), ("turn", "residual"), ("project",)), 1: (("apply",), (), ("spread",)),
                       2: ((), ("hidden0",), ("hidden1",)), 3: ((), ("hidden2",), ("hidden3",))},
                      {0: ((), ("hidden4",), ()), 1: (("apply2",), (), ("out",)), 3: ((), ("conv",), ())}),
            "self": ({2: ((), ("turn", "residual"), ("project",)), 3: (("apply",), (), ("spread",))},
                     {0: ((), (), ("pool",))})}
        ends_narrow = {
            "cross": ({0: ((), ("turn",), ("project",)), 1: (("apply",), (), ("spread",)),
                       2: ((), ("hidden0",), ("hidden1",)), 3: ((), ("hidden2",), ("hidden3",))},
                      {0: ((), ("hidden4",), ()), 1: (("apply2",), ("out",), ()), 2: ((), ("conv",), ())}),
            "self": ({0: ((), ("turn",), ("project",)), 1: (("apply",), (), ("spread",)), 2: ((), ("pool",), ())},
                     {})}
        starts_mixed = {0: (("queries",), ("masks_hi",)), 1: (("keys",), ("masks_lo",)),
                        2: (("values",), ("take_values",))}
        starts_narrow = {0: ((), ("queries", "masks_hi")), 1: (("keys",), ("masks_lo",)),
                         2: (("values",), ("take_values",))}

        def run_unit(do, u, older, before, after, narrow):
            starts = starts_narrow if narrow else starts_mixed
            tables = ends_narrow if narrow else ends_mixed

            def ends(k, place):
                for unit_of, distance in ((older, 1), (before, 0)):
                    if unit_of is not None:
                        for stage in tables[unit_of.kind][distance].get(k, ((), (), ()))[place]:
                            if stage != "conv":
                                do(stage, unit_of)
                            elif not narrow and not (type(unit_of.i) is int and unit_of.i + unit_of.half == 0):
                                do("conv", unit_of, unit_of.i * 2 + (unit_of.half - 1))
                            elif narrow and unit_of.half == 1:
                                do("conv", unit_of, unit_of.i)

            for k in range(u.pairs):
                nxt = pair_at((u, after), k + 1)
                over = pair_at((u, after), k + 2)
                ends(k, 0)
                if nxt:
                    do("scores", *nxt)
                if over:
                    do("rough", *over)
                if after and k == 0:
                    do("gather", after)
                if after:
                    for stage in starts.get(k, ((), ()))[0]:
                        do(stage, after)
                ends(k, 1)
                do("weigh", u, k)
                ends(k, 2)
                if after:
                    for stage in starts.get(k, ((), ()))[1]:
                        do(stage, after)
                if narrow and k == u.pairs - 1:
                    do("residual", u)

        def unit(kind, half, par, no, body, crosses, image, i):
            return Unit(kind, half, par, no, LPAIRS if kind == "low" else PAIRS, body, crosses, image, i)

        def strips_of_image(do, fori, low, units_at):
            def body(i):
                units = units_at(i)
                earlier = units_at(i - 1)[-2:] if not (type(i) is int and i == 0) else [None, None]
                later = units_at(i + 1)[0] if not (type(i) is int and i == PER - 1) else None
                row = earlier + units + [later]
                for n in range(2, len(row) - 1):
                    run_unit(do, row[n], row[n - 2], row[n - 1], row[n + 1], len(units) == 2)

            head(do, units_at(0)[0], low)
            body(0)
            with fori(0, PER - 2) as i:
                body(i + 1)
            body(PER - 1)
            return units_at(PER - 1)[-2:]

        def finish(do, older, last, low):
            if last.kind == "self":
                for stage in ("turn", "project", "apply", "spread", "pool"):
                    do(stage, last)
                ends = []
            elif low is not None:
                do("pool", older)
                do("turn", last)
                ends = ["project", "apply", "spread", "hidden0", "hidden1", "hidden2", "hidden3", "hidden4"]
                do("residual", last)
            else:
                do("turn", last)
                do("hidden4", older)
                do("project", last)
                do("apply2", older)
                do("conv", older, PER - 1)
                do("out", older)
                do("apply", last)
                do("conv", older, PER)
                do("spread", last)
                do("conv", older, PER + 1)
                for stage in ("hidden0", "hidden1", "hidden2", "hidden3", "hidden4", "apply2", "out"):
                    do(stage, last)
                for strip in range(2 * PER - 2, STRIPS):
                    do("conv", last, strip)
                return

            def end():
                if ends:
                    do(ends.pop(0), last)

            do("make_low", low)
            do("queries", low)
            do("masks_hi", low)
            end()
            end()
            do("keys", low)
            do("masks_lo", low)
            end()
            do("values", low)
            do("take_values", low)
            end()
            do("rough", low, 0)
            end()
            do("scores", low, 0)
            do("rough", low, 1)
            end()
            do("scores", low, 1)
            end()
            do("weigh", low, 0)
            end()
            do("weigh", low, 1)
            if last.kind == "cross":
                do("apply2", last)
                do("out", last)
            do("turn", low)
            do("residual", low)
            if last.kind == "cross":
                do("conv", last, STRIPS - 2)
            do("project", low)
            if last.kind == "cross":
                do("conv", last, STRIPS - 1)

        def walk(fori, do):
            per_image = 2 * STRIPS + 1
            older, last = strips_of_image(do, fori, None, lambda i: [
                unit("self", h, h, i * 2 + h, i, 0, 0, i) for h in range(2)])
            low = unit("low", 0, 0, STRIPS, 0, 0, 0, 0)
            finish(do, older, last, low)
            with fori(0, IMAGES - 1) as n:
                def pairs_of_units(i):
                    no = n * per_image + (i * 4 + (STRIPS + 1))
                    bc = n * PER + i
                    return [unit("self" if u % 2 == 0 else "cross", u // 2, u % 2, no + u,
                                 bc + PER if u % 2 == 0 else bc, bc * 2 + u // 2, n, i) for u in range(4)]
                low = unit("low", 0, 0, n * per_image + STRIPS, n, n * STRIPS, n, 0)
                older, last = strips_of_image(do, fori, low, pairs_of_units)
                finish(do, older, last, unit("low", 0, 0, n * per_image + (3 * STRIPS + 1), n + 1,
                                             n * STRIPS + STRIPS, n, 0))
            low = unit("low", 0, 0, (IMAGES - 1) * per_image + STRIPS, IMAGES - 1, (IMAGES - 1) * STRIPS,
                       IMAGES - 1, 0)
            older, last = strips_of_image(do, fori, low, lambda i: [
                unit("cross", h, h, i * 2 + (h + STRIPS + 1 + (IMAGES - 1) * per_image), i + (IMAGES - 1) * PER,
                     (i + (IMAGES - 1) * PER) * 2 + h, IMAGES - 1, i) for h in range(2)])
            finish(do, older, last, None)

        def convolved(u):
            if type(u.image) is int:
                return u.image * STRIPS + (2 * PER - 2 if type(u.i) is int and u.i * 2 + u.half == STRIPS - 1 else u.i)
            if type(u.i) is int and u.i == 0:
                return u.image * STRIPS
            return u.image * STRIPS + (u.i * 2 + (u.half - 1))

        def telling(stages):
            return lambda stage, *what: stages[stage](*what) if stage in stages else None

        def loads_after(u):
            if u.kind == "low" or (type(u.no) is int and u.no < 2):
                return None
            narrow = type(u.image) is int
            if type(u.i) is int and u.i == 0:
                return u.no - (1 if narrow else 2)
            return u.no - (1 if narrow else 3)

        def step(u):
            return PAIRS // u.pairs

        def pair_no(u, k):
            return u.no * PAIRS + k * step(u)

        def query_source(u):
            return xlow[:, :] if u.kind == "low" else (xself if u.kind == "self" else xcross)[:, u.half, :]

        def key_source(u):
            return xpatch[:, u.half, :] if u.kind == "cross" else query_source(u)

        def which(u):
            return 1 if u.kind == "cross" else 0

        block = ctx.enter_context(nc.Block())

        setup_loads = []
        for m in range(2):
            setup_loads += [(wq_sb[:, m, :], wq[m]), (wk_sb[:, m, :], wk[m]), (wv_sb[:, m, :], wv[m])]
            setup_loads += [(wf_sb[64 * h2:64 * h2 + 64, m, :], wf[m][h2]) for h2 in range(2)]
        setup_loads += [
            (w1_sb[:, :], w1), (w2_sb[:, :, :], w2.rearrange("(b f) n -> f b n", b=FB)), (b1_sb[:, :], b1),
            (gain[:, :], gains), (shift[:, :], shifts), (bn_sb[:, :], bn), (ident[:, :], consts[:, 0:128]),
            (headmask[:, :], consts[:, 128:132]), (half_neg[:, :], consts[:, 132:136]),
            (eps[:, :], consts[:, 264:268]),
            (ones2_f[:, :], consts[0:2, 136:264]), (brow_f[:, :], bias_rows),
            (hid[:, 0:3, :].rearrange("p a b -> p (a b)")[:, 0:TAPS * C], convw)]

        @block.sync
        def _(sp):
            for to, src in setup_loads:
                sp.dma_start(to, src).then_inc(s_setup, 16)
            sp.wait_ge(s_prep_v, 2)
            for r in range(PAIRS):
                for part, src in ((0, brow_hi), (1, brow_lo)):
                    sp.dma_start(brow[part:part + 1, :, r, :],
                                 src[:, :].rearrange("p (a c) -> p a c", a=3)).then_inc(s_brow, 16)

            def load_tokens(u):
                strip = bass.ds(u.body * 2 + u.half, 1)
                if loads_after(u) is not None:
                    sp.wait_ge(s_resid, loads_after(u))
                if u.kind == "self":
                    sp.dma_start(xself[:, u.half, :], x[strip, :, :].rearrange("a c t -> (a c) t")
                                 ).then_inc(s_xself_in[u.half], 16)
                if u.kind == "cross":
                    sp.wait_ge(s_self_stored[u.half], u.body * 16 + 16)
                    sp.dma_start(xcross[:, u.half, :], self_out[strip, :, :].rearrange("a c t -> (a c) t")
                                 ).then_inc(s_xcross[u.half], 16)

            walk(nc.sync.Fori, telling({"queries": load_tokens}))

            for h in range(2):
                sp.wait_ge(s_x2_stored[h], 16 * IMAGES * PER)
            def chunk(dram, image, q):
                return dram[bass.ds(image, 1), :, q * CHUNK:(q + 1) * CHUNK].rearrange("a c t -> (a c) t")

            def load(image, q):
                sp.wait_ge(s_last_out[q], image * 16)
                sp.dma_start(lastx[:, q, :], chunk(ffn_out, image, q)).then_inc(s_last_in[q], 16)

            def store(image, q):
                sp.wait_ge(s_sum, image * CHUNKS + q + 1)
                sp.dma_start(chunk(out, image, q), lastx[:, q, :]).then_inc(s_last_out[q], 16)

            for q in range(CHUNKS):
                load(0, q)
            with nc.sync.Fori(0, IMAGES - 1) as i:
                for q in range(CHUNKS + 1):
                    if q < CHUNKS:
                        store(i, q)
                    if q:
                        load(i + 1, q - 1)
            for q in range(CHUNKS):
                store(IMAGES - 1, q)
            for q in range(CHUNKS):
                sp.wait_ge(s_last_out[q], 16 * IMAGES)

        @block.tensor
        def _(pe):
            mm = nc.tensor.matmul

            def project(u, kind):
                w = (wq_sb if kind == "q" else wk_sb)[:, which(u), :]
                src = (query_source(u) if kind == "q" else key_source(u)).rearrange(
                    "c (p w t) -> c p w t", w=2, t=TOK)
                n = u.pairs * TOK
                for g in range(2):
                    for win in range(2):
                        last = mm(ps_proj[64 * win:64 * win + 64, g * n:(g + 1) * n], w[:, 64 * g:64 * g + 64],
                                  src[:, :, win, :], start=True, stop=True, skip_group_check=True)
                last.then_inc(s_q if kind == "q" else s_k, 1)

            def project_q(u):
                if u.kind == "self":
                    pe.wait_ge(s_xself_in[u.half], u.body * 16 + 16)
                elif u.kind == "cross":
                    pe.wait_ge(s_xcross[u.half], u.body * 16 + 16)
                else:
                    pe.wait_ge(s_xlow, u.body + 1)
                pe.wait_ge(s_proj_free, u.no * 3)
                project(u, "q")

            def project_k(u):
                if u.kind == "cross":
                    pe.wait_ge(s_xpatch, u.body * 2 + (u.half + 1))
                pe.wait_ge(s_proj_free, u.no * 3 + 1)
                project(u, "k")

            def project_v(u):
                pe.wait_ge(s_proj_free, u.no * 3 + 2)
                src = key_source(u)
                for p in range(u.pairs):
                    last = mm(ps_proj[:, C * p:C * p + C], src[:, C * p:C * p + C], wv_sb[:, which(u), :],
                              start=True, stop=True, skip_group_check=True)
                last.then_inc(s_v, 1)

            def rough_scores(u, k):
                if k == 0:
                    pe.wait_ge(s_qm_hi, u.no + 1)
                    pe.wait_ge(s_khi, u.no + 1)
                for j in range(4):
                    a = (j // 2) * u.pairs + k
                    last = mm(ps_max[:, 128 * j:128 * j + 128],
                              qm_hi[:, u.par, a, 2 * (j % 2):2 * (j % 2) + 2, :].rearrange("p h t -> p (h t)"),
                              ks_hi[:, u.par, a, :, :].rearrange("p w t -> p (w t)"),
                              start=True, stop=True, skip_group_check=True)
                last.then_inc(s_max, step(u))

            def scores(u, k):
                ps = ps_s
                pe.wait_ge(s_prob, pair_no(u, k))
                if k == 0:
                    pe.wait_ge(s_qm_lo, u.no + 1)
                    pe.wait_ge(s_proj_free, u.no * 3 + 2)
                for g in range(2):
                    a = g * u.pairs + k
                    for n, (kk, qq) in enumerate(((ks_hi, qm_hi), (ks_hi, qm_lo), (ks_lo, qm_hi))):
                        mm(ps[:, 256 * g:256 * g + 256], kk[:, u.par, a, :, :].rearrange("p w t -> p (w t)"),
                           qq[:, u.par, a, :, :].rearrange("p h t -> p (h t)"),
                           start=(g == 0 and n == 0), stop=False, skip_group_check=True)
                pe.wait_ge(s_negb, pair_no(u, k) + step(u))
                for j in range(4):
                    last = mm(ps[:, 128 * j:128 * j + 128],
                              negmax_b[:, k % 2, 2 * j:2 * j + 2, :].rearrange("p w t -> p (w t)"),
                              identb[:, :], start=False, stop=True, skip_group_check=True)
                last.then_inc(s_s, step(u))

            def weigh(u, k):
                if k == 0:
                    pe.wait_ge(s_proj_free, u.no * 3 + 3)
                pe.wait_ge(s_prob, pair_no(u, k) + step(u))
                pe.wait_ge(s_on, pair_no(u, k))
                for j in range(4):
                    last = mm(ps_o[:, VC * j:VC * j + VC], prob[:, k % 2, 128 * j:128 * j + 128],
                              vb[:, u.par, 4 * k + j, :], start=True, stop=True, skip_group_check=True)
                last.then_inc(s_pv, step(u))

            def turn_heads(u):
                pe.wait_ge(s_on, u.no * PAIRS + PAIRS)
                pe.wait_ge(s_xt_out, u.no)
                pe.wait_ge(s_sign, u.crosses - 1 if u.kind == "cross" and type(u.image) is int else u.crosses)
                for p in range(u.pairs):
                    last = mm(ps_t[:, C * p:C * p + C], onorm[:, u.par, p, :], ident[:, :], is_transpose=True,
                              start=True, stop=True, skip_group_check=True)
                last.then_inc(s_ot, 1)

            def residual(ps, pairs, src, bias):
                for p in range(pairs):
                    mm(ps[:, C * p:C * p + C], src[:, C * p:C * p + C], ident[:, :], is_transpose=True,
                       start=(p == 0), stop=False, skip_group_check=True)
                return mm(ps[:, 0:C * pairs], ones2[:, :],
                          brow[:, bias, 0:pairs, :].rearrange("p a c -> p (a c)"), start=False, stop=False,
                          skip_group_check=True)

            def attention_residual(u):
                pe.wait_ge(s_xn, pair_no(u, 0))
                residual(ps_y, u.pairs, query_source(u), which(u)).then_inc(s_resid, 1)

            def project_out(u):
                pe.wait_ge(s_oT, u.no + 1)
                for p in range(u.pairs):
                    last = mm(ps_y[:, C * p:C * p + C], oT[:, C * p:C * p + C], wf_sb[:, which(u), :],
                              start=False, stop=True, skip_group_check=True)
                last.then_inc(s_y, 1)

            def turn_tokens(src, pairs, normalised, count_at, done):
                for p in range(pairs):
                    pe.wait_ge(normalised, count_at(p))
                    last = mm(ps_t[:, C * p:C * p + C], src[:, C * p:C * p + C], ident[:, :], is_transpose=True,
                              start=True, stop=True, skip_group_check=True)
                last.then_inc(done, 1)

            def spread(u):
                pe.wait_ge(s_sign, u.crosses)
                turn_tokens(xn, u.pairs, s_xn, lambda p: pair_no(u, p) + step(u), s_xt)

            def hidden(u, b):
                if b == 0:
                    pe.wait_ge(s_xt_out, u.no + 1)
                    pe.wait_ge(s_yconv, convolved(u))
                pe.wait_ge(s_relu, u.crosses * FB + b)
                if b < FB:
                    mm(ps_hid[:, :], w1_sb[:, C * b:C * b + C], xf[:, :], start=True, stop=True,
                       skip_group_check=True).then_inc(s_hid, 1)
                if b == 0:
                    pe.wait_ge(s_xn2, u.crosses * PAIRS)
                    residual(ps_y2, PAIRS, xf, 2)
                else:
                    for p in range(PAIRS):
                        last = mm(ps_y2[:, C * p:C * p + C], hid[:, b - 1, C * p:C * p + C], w2_sb[:, b - 1, :],
                                  start=False, stop=(b == FB), skip_group_check=True)
                if b == FB:
                    last.then_inc(s_y2, 1)

            def turn_out(u):
                turn_tokens(xn2, PAIRS, s_xn2, lambda p: u.crosses * PAIRS + p + 1, s_xt2)

            def conv(u, strip):
                pe.wait_ge(s_sign, u.image * STRIPS + (strip + (1 if type(strip) is int and strip == STRIPS - 1 else 2)))
                pe.wait_ge(s_relu, u.crosses * FB + FB)
                pe.wait_ge(s_yconv, u.image * STRIPS + strip)
                for t in range(TAPS):
                    dy, dx = t // 3, t % 3
                    last = mm(ps_hid[:, :].rearrange("p (r w) -> p r w", r=WIN), convs[:, t, :],
                              smap[:, bass.ds(strip * WIN + dy, WIN), dx:dx + W],
                              start=(t == 0), stop=(t == TAPS - 1), skip_group_check=True)
                last.then_inc(s_conv, 1)

            pe.wait_ge(s_setup, 16 * len(setup_loads))
            pe.wait_ge(s_brow, 16 * 2 * PAIRS)
            pe.wait_ge(s_prep_v, 3)
            pe.wait_ge(s_prep_a, 1)
            pe.wait_ge(s_prep_g, 2)

            walk(nc.tensor.Fori, telling({
                "queries": project_q, "keys": project_k, "values": project_v, "rough": rough_scores,
                "scores": scores, "weigh": weigh, "turn": turn_heads, "residual": attention_residual,
                "project": project_out, "spread": spread,
                "hidden0": lambda u: hidden(u, 0), "hidden1": lambda u: hidden(u, 1),
                "hidden2": lambda u: hidden(u, 2), "hidden3": lambda u: hidden(u, 3),
                "hidden4": lambda u: hidden(u, 4),
                "out": turn_out, "conv": conv}))

        @block.scalar
        def _(act):
            activation = nc.scalar.activation

            def take_q(u):
                act.wait_ge(s_q, u.no + 1)
                a = 2 * u.pairs
                activation(qc_hi[:, 0:a * TOK], ps_proj[:, 0:a * TOK], ACT.Identity, scale=QS).then_inc(s_qhi, 1)

            def mask_q_hi(u):
                a = 2 * u.pairs
                act.wait_ge(s_qhi, u.no + 1)
                for h in range(4):
                    last = activation(qm_hi[:, u.par, 0:a, h, :],
                                      qc_hi[:, 0:a * TOK].rearrange("p (a t) -> p a t", a=a), ACT.Identity,
                                      scale=headmask[:, h:h + 1])
                last.then_inc(s_qm_hi, 1)

            def take_k(u):
                act.wait_ge(s_k, u.no + 1)
                a = 2 * u.pairs
                for win in range(2):
                    r = slice(64 * win, 64 * win + 64)
                    last = activation(ks_hi[r, u.par, 0:a, win, :],
                                      ps_proj[r, 0:a * TOK].rearrange("p (a t) -> p a t", a=a), ACT.Identity)
                last.then_inc(s_khi, 1)

            def take_v(u):
                act.wait_ge(s_v, u.no + 1)
                a = 4 * u.pairs
                for win in range(2):
                    r = slice(64 * win, 64 * win + 64)
                    last = activation(vb[r, u.par, 0:a, 32 * win:32 * win + 32],
                                      ps_proj[r, 0:a * 32].rearrange("p (a t) -> p a t", a=a), ACT.Identity)
                last.then_inc(s_proj_free, 1)

            def exponentials(u, k):
                act.wait_ge(s_s, pair_no(u, k) + step(u))
                activation(prob[:, k % 2, :], ps_s[:, :], ACT.Exp).then_inc(s_prob, step(u))

            def take_turned(u):
                act.wait_ge(s_ot, u.no + 1)
                n = u.pairs * C
                src = ps_t[:, 0:n].rearrange("p (a h t) -> p a h t", h=2, t=TOK)
                to = oT[:, 0:n].rearrange("p (a w t) -> p a w t", w=2, t=TOK)
                for win in range(2):
                    for h2 in range(2):
                        last = activation(to[64 * h2:64 * h2 + 64, :, win, :], src[64 * win:64 * win + 64, :, h2, :],
                                          ACT.Identity)
                last.then_inc(s_oT, 1)

            def take_output(u):
                act.wait_ge(s_xt, u.no + 1)
                if u.kind == "self":
                    act.wait_ge(s_self_stored[u.half], u.body * 16)
                    act.wait_ge(s_colsum, u.body * 2 + u.half)
                    to = xa[:, u.half, :]
                elif u.kind == "cross":
                    to = xf[:, :]
                else:
                    act.wait_ge(s_kv0, u.body)
                    to = low_out[:, :]
                m = which(u)
                activation(to, ps_t[:, 0:u.pairs * C], ACT.Identity, bias=shift[:, m:m + 1],
                           scale=gain[:, m:m + 1]).then_inc(s_xt_out, 1)

            def store_self(u):
                act.wait_ge(s_xt_out, u.no + 1)
                act.dma_start(self_out[bass.ds(u.body * 2 + u.half, 1), :, :].rearrange("a c t -> (a c) t"),
                              xa[:, u.half, :]).then_inc(s_self_stored[u.half], 16)

            def take_hidden(u, b):
                act.wait_ge(s_hid, u.crosses * FB + b + 1)
                activation(hid[:, b, :], ps_hid[:, :], ACT.Relu, bias=b1_sb[:, b:b + 1]).then_inc(s_relu, 1)

            def take_out(u):
                act.wait_ge(s_xt2, u.crosses + 1)
                act.wait_ge(s_x2_stored[u.half], u.body * 16)
                src = ps_t[:, :].rearrange("p (v r w) -> p v r w", v=WIN, r=WIN)
                activation(x2[:, u.half, :].rearrange("p (r v w) -> p v r w", r=WIN, v=WIN), src, ACT.Identity,
                           bias=shift[:, 2:3], scale=gain[:, 2:3]).then_inc(s_x2, 1)
                act.wait_ge(s_conv, u.image * STRIPS)
                rows = smap[:, bass.ds(u.i * 2 * WIN + (u.half * WIN + 1), WIN), 1:1 + W]
                activation(rows.rearrange("p r (v w) -> p v r w", v=WIN), src, ACT.Sign,
                           bias=shift[:, 2:3], scale=gain[:, 2:3]).then_inc(s_sign, 1)
                act.wait_ge(s_x2, u.crosses + 1)
                act.dma_start(ffn_out[bass.ds(u.image, 1), :, bass.ds(u.i * 2 * SW + u.half * SW, SW)
                                      ].rearrange("a c t -> (a c) t"),
                              x2[:, u.half, :]).then_inc(s_x2_stored[u.half], 16)

            def take_conv(u, strip):
                act.wait_ge(s_conv, u.image * STRIPS + (strip + 1))
                activation(yconv[:, bass.ds(u.image * H * W + strip * SW, SW)], ps_hid[:, :], ACT.Identity
                           ).then_inc(s_yconv, 1)

            act.wait_ge(s_setup, 16 * len(setup_loads))
            activation(convs[:, :, :].rearrange("p a b -> p (a b)"),
                       hid[:, 0:3, :].rearrange("p a b -> p (a b)")[:, 0:TAPS * C], ACT.Sign).then_inc(s_prep_a, 1)
            act.wait_ge(s_prep_v, 3)
            act.wait_ge(s_prep_g, 2)
            act.wait_ge(s_prep_a, 1)

            walk(nc.scalar.Fori, telling({
                "queries": take_q, "masks_hi": mask_q_hi, "keys": take_k, "take_values": take_v, "scores": exponentials, "turn": take_turned,
                "spread": take_output, "hidden0": lambda u: take_hidden(u, 0),
                "hidden1": lambda u: take_hidden(u, 1), "hidden2": lambda u: take_hidden(u, 2),
                "hidden3": lambda u: take_hidden(u, 3), "pool": store_self, "out": take_out,
                "conv": take_conv}))

            act.wait_ge(s_bnab, 3)
            with nc.scalar.Fori(0, IMAGES) as i:
                for q in range(CHUNKS):
                    act.wait_ge(s_sum, i * CHUNKS + (q - 1) if q else i * CHUNKS)
                    activation(lasty[:, q % 2, :], yconv[:, bass.ds(i * H * W + q * CHUNK, CHUNK)], ACT.Identity,
                               bias=bnv[:, 6:7], scale=bnv[:, 4:5]).then_inc(s_affine, 1)

        @block.vector
        def _(dve):
            v = nc.vector

            def split_q(u):
                dve.wait_ge(s_qhi, u.no + 1)
                a = 2 * u.pairs
                v.scalar_tensor_tensor(out=qc_lo[:, 0:a * TOK], in0=ps_proj[:, 0:a * TOK], scalar=QS,
                                       in1=qc_hi[:, 0:a * TOK], op0=ALU.mult, op1=ALU.subtract
                                       ).then_inc(s_proj_free, 1)

            def mask_q_lo(u):
                a = 2 * u.pairs
                dve.wait_ge(s_proj_free, u.no * 3 + 1)
                for h in range(4):
                    last = v.tensor_scalar(qm_lo[:, u.par, 0:a, h, :],
                                           qc_lo[:, 0:a * TOK].rearrange("p (a t) -> p a t", a=a),
                                           headmask[:, h:h + 1], None, ALU.mult)
                last.then_inc(s_qm_lo, 1)

            def split_k(u):
                dve.wait_ge(s_khi, u.no + 1)
                a = 2 * u.pairs
                for win in range(2):
                    r = slice(64 * win, 64 * win + 64)
                    last = v.tensor_tensor(ks_lo[r, u.par, 0:a, win, :],
                                           ps_proj[r, 0:a * TOK].rearrange("p (a t) -> p a t", a=a),
                                           ks_hi[r, u.par, 0:a, win, :], ALU.subtract)
                last.then_inc(s_proj_free, 1)

            def maxima(u, k):
                dve.wait_ge(s_max, pair_no(u, k) + step(u))
                v.tensor_reduce(negmax[:, k % 2, :], ps_max[:, :].rearrange("p (a t) -> p a t", t=TOK), AX.X,
                                ALU.max, negate=True).then_inc(s_neg, step(u))
                dve.wait_ge(s_neg, pair_no(u, k) + step(u))
                v.tensor_copy(negmax_b[:, k % 2, :, :],
                              negmax[:, k % 2, :].unsqueeze(2).to_broadcast([128, 8, TOK])
                              ).then_inc(s_negb, step(u))

            def normalise(u, k):
                dve.wait_ge(s_pv, pair_no(u, k) + step(u))
                blocks = ps_o[:, 0:4 * VC].rearrange("p (j c) -> p j c", j=4)
                v.reciprocal(rden[:, k % 2, :, :], blocks[:, :, 64:66]).then_inc(s_rden, step(u))
                dve.wait_ge(s_rden, pair_no(u, k) + step(u))
                for h2 in range(2):
                    r = slice(64 * h2, 64 * h2 + 64)
                    last = v.tensor_tensor(
                        onorm[r, u.par, k, :].rearrange("p (w j d) -> p j w d", w=2, j=4),
                        blocks[r, :, 0:64].rearrange("p j (w h d) -> p j w h d", w=2, h=2)[:, :, :, h2, :],
                        rden[r, k % 2, :, :].unsqueeze(3).to_broadcast([64, 4, 2, DH]), ALU.mult)
                last.then_inc(s_on, step(u))

            def norm_stats(ps, to, mean_var, pairs, done, count, stats_done, mv_done):
                dve.wait_ge(done, count)
                for p in range(pairs):
                    last = v.bn_stats(to[:, p, :], ps[:, C * p:C * p + C])
                last.then_inc(stats_done, 1)
                dve.wait_ge(stats_done, count)
                dve.sem_inc(s_aggr, 1)
                for p in range(pairs):
                    last = v.bn_aggr(mean_var[:, p, :], to[:, p, :])
                last.then_inc(mv_done, 1)

            def norm_apply(ps, to, mean_var, factor, pairs, count, rstd_done, done, by):
                dve.wait_ge(rstd_done, count)
                for p in range(pairs):
                    v.tensor_scalar(to[:, C * p:C * p + C], ps[:, C * p:C * p + C], mean_var[:, p, 0:1],
                                    factor[:, p:p + 1], ALU.subtract, ALU.mult).then_inc(done, by)

            def stats_of(u):
                norm_stats(ps_y, stats, mv, u.pairs, s_y, u.no + 1, s_stats, s_mv)

            def apply_to(u):
                norm_apply(ps_y, xn, mv, rstd, u.pairs, u.no + 1, s_rstd, s_xn, step(u))

            def stats2_of(u):
                norm_stats(ps_y2, stats2, mv2, PAIRS, s_y2, u.crosses + 1, s_stats2, s_mv2)

            def apply2_to(u):
                norm_apply(ps_y2, xn2, mv2, rstd2, PAIRS, u.crosses + 1, s_rstd2, s_xn2, 1)

            def pool(u):
                strip = u.body * 2 + u.half
                dve.wait_ge(s_xt_out, u.no + 1)
                dve.wait_ge(s_pooled, strip)
                v.tensor_reduce(colsum[:, :], xa[:, u.half, :].rearrange("p (a f) -> p a f", f=DOWN), AX.X,
                                ALU.add).then_inc(s_colsum, 1)
                dve.wait_ge(s_colsum, strip + 1)
                v.tensor_reduce(low_sum[:, bass.ds(u.i * 2 + u.half, 1), :].rearrange("p a (w c) -> p (a w) c", c=2),
                                colsum[:, :].rearrange("p (w r c) -> p w c r", r=DOWN, c=2), AX.X,
                                ALU.add).then_inc(s_pooled, 1)

            def make_low(low):
                dve.wait_ge(s_pooled, low.body * STRIPS + STRIPS)
                q = LH // WIN
                for wi in range(q):
                    last = v.tensor_scalar(
                        xlow[:, :].rearrange("p (a b s t) -> p a b s t", a=q, b=q, s=4)[:, wi, :, :, :],
                        low_sum[:, 4 * wi:4 * wi + 4, :].rearrange("p s (b t) -> p b s t", b=q),
                        1.0 / (DOWN * DOWN), None, ALU.mult)
                last.then_inc(s_xlow, 1)

            def pad_low(low):
                dve.wait_ge(s_xt_out, low.no + 1)
                dve.wait_ge(s_xpatch, low.body * STRIPS)
                q = LH // WIN
                for wi in range(q):
                    for wj in range(q):
                        src = low_out[:, :].rearrange("p (a s v r c) -> p a s v r c", a=q * q, s=4, v=4, r=2)
                        for r in range(2):
                            rows = kvpad[:, WIN * wi:WIN * wi + WIN, WIN * wj:WIN * wj + WIN]
                            last = v.tensor_copy(
                                rows.rearrange("p (s r) (v c) -> p s r v c", r=2, c=2)[:, :, r, :, :],
                                src[:, q * wi + wj, :, :, r, :])
                last.then_inc(s_kv0, 1)
                dve.wait_ge(s_kv0, low.body + 1)
                v.tensor_copy(kvpad[:, 0:LH, LH:KP], kvpad[:, 0:LH, 0:KP - LH]).then_inc(s_kv1, 1)
                dve.wait_ge(s_kv1, low.body + 1)
                v.tensor_copy(kvpad[:, LH:KP, :], kvpad[:, 0:KP - LH, :]).then_inc(s_kv, 1)

            def conv_stats(u, strip):
                dve.wait_ge(s_yconv, u.image * STRIPS + (strip + 1))
                v.bn_stats(ystats[:, bass.ds(u.image * STRIPS + strip, 1), :].rearrange("p a b -> p (a b)"),
                           yconv[:, bass.ds(u.image * H * W + strip * SW, SW)]).then_inc(s_ystats, 1)

            dve.wait_ge(s_setup, 16 * len(setup_loads))
            v.tensor_copy(brow_hi[:, :], brow_f[:, :]).then_inc(s_prep_v, 1)
            dve.wait_ge(s_prep_v, 1)
            v.tensor_tensor(brow_lo[:, :], brow_f[:, :], brow_hi[:, :], ALU.subtract).then_inc(s_prep_v, 1)
            v.tensor_copy(ones2[:, :], ones2_f[:, :])
            v.tensor_copy(identb[:, :], ident[:, :])
            v.memset(ks_hi[:, :, :, :, :], 0.0)
            v.memset(ks_lo[:, :, :, :, :], 0.0).then_inc(s_prep_v, 1)
            dve.wait_ge(s_prep_v, 3)
            dve.wait_ge(s_prep_g, 2)

            walk(nc.vector.Fori, telling({
                "queries": split_q, "masks_lo": mask_q_lo, "keys": split_k, "rough": maxima, "weigh": normalise, "project": stats_of,
                "apply": apply_to, "hidden4": stats2_of, "apply2": apply2_to, "pool": pool, "make_low": make_low,
                "pad_low": pad_low, "conv": conv_stats}))

            dve.wait_ge(s_ystats, IMAGES * STRIPS)
            v.bn_aggr(bnv[:, 0:2], ystats[:, :, :].rearrange("p a b -> p (a b)")).then_inc(s_bn, 1)
            dve.wait_ge(s_bnr, 2)
            v.tensor_tensor(bnv[:, 4:5], bnv[:, 3:4], bn_sb[:, 0:1], ALU.mult).then_inc(s_bnab, 1)
            dve.wait_ge(s_bnab, 1)
            v.tensor_tensor(bnv[:, 5:6], bnv[:, 0:1], bnv[:, 4:5], ALU.mult).then_inc(s_bnab, 1)
            dve.wait_ge(s_bnab, 2)
            v.tensor_tensor(bnv[:, 6:7], bn_sb[:, 1:2], bnv[:, 5:6], ALU.subtract).then_inc(s_bnab, 1)
            with nc.vector.Fori(0, IMAGES) as i:
                for q in range(CHUNKS):
                    dve.wait_ge(s_last_in[q], i * 16 + 16)
                    dve.wait_ge(s_affine, i * CHUNKS + q + 1)
                    v.tensor_tensor(lastx[:, q, :], lastx[:, q, :], lasty[:, q % 2, :], ALU.add).then_inc(s_sum, 1)

        @block.gpsimd
        def _(pool):
            g = nc.gpsimd

            def inv_sqrt(var, var_eps, to, pairs, count, mv_done, var_done, rstd_done):
                pool.wait_ge(mv_done, count)
                g.tensor_tensor(var_eps[:, 0:pairs], var[:, 0:pairs, 1], eps[:, 0:pairs], ALU.add
                                ).then_inc(var_done, 1)
                pool.wait_ge(var_done, count)
                g.tensor_tensor(to[:, 0:pairs], var_eps[:, 0:pairs], half_neg[:, 0:pairs], ALU.pow
                                ).then_inc(rstd_done, 1)

            def rstd_of(u):
                inv_sqrt(mv, vareps, rstd, u.pairs, u.no + 1, s_mv, s_var, s_rstd)

            def rstd2_of(u):
                inv_sqrt(mv2, vareps2, rstd2, PAIRS, u.crosses + 1, s_mv2, s_var2, s_rstd2)

            def gather(u):
                if u.kind != "cross":
                    return
                pool.wait_ge(s_kv, u.image + 1)
                pool.wait_ge(s_resid, loads_after(u))
                pool.sem_inc(s_gather, 1)
                rows = kvpad[:, bass.ds(u.i * 2 * STRIDE + u.half * STRIDE, WIN), :]
                for win in range(STRIPS):
                    last = g.tensor_copy(
                        xpatch[:, u.half, TOK * win:TOK * win + TOK].rearrange("p (r c) -> p r c", r=WIN),
                        rows[:, :, STRIDE * win:STRIDE * win + WIN])
                last.then_inc(s_xpatch, 1)

            pool.wait_ge(s_setup, 16 * len(setup_loads))
            g.memset(smap[:, :, :], 0.0)
            g.memset(vb[:, :, :, :], 0.0).then_inc(s_prep_g, 1)
            pool.wait_ge(s_prep_g, 1)
            for win in range(2):
                last = g.memset(vb[64 * win:64 * win + 64, :, :, 64 + win:65 + win], 1.0)
            last.then_inc(s_prep_g, 1)

            walk(nc.gpsimd.Fori, telling({"gather": gather, "project": rstd_of, "hidden4": rstd2_of}))
            pool.wait_ge(s_bn, 1)
            g.tensor_tensor(bnv[:, 2:3], bnv[:, 1:2], eps[:, 0:1], ALU.add).then_inc(s_bnr, 1)
            pool.wait_ge(s_bnr, 1)
            g.tensor_tensor(bnv[:, 3:4], bnv[:, 2:3], half_neg[:, 0:1], ALU.pow).then_inc(s_bnr, 1)


def kernel(**inputs):
    import numpy as np
    import concourse.bacc as bacc
    from concourse.bass_utils import run_bass_kernel_spmd

    a = {k: np.asarray(t) for k, t in inputs.items()}
    L0 = {k[len("L0_conv_"):]: t for k, t in a.items() if k.startswith("L0_conv_")}
    both = lambda name: np.stack([L0["sa_" + name], L0["ca_" + name]])
    consts = np.zeros((128, 268), np.float32)
    consts[:, 0:128] = np.eye(128)
    for h in range(4):
        for win in range(2):
            consts[win * 64 + h * DH:win * 64 + h * DH + DH, 128 + h] = 1.0
    consts[:, 132:136] = -0.5
    consts[:, 136:264] = 1.0
    consts[:, 264:268] = EPS
    arrays = {
        "x": a["x"].reshape(IMAGES, C, STRIPS, WIN, W // WIN, WIN).transpose(0, 2, 1, 4, 3, 5
                                                                             ).reshape(IMAGES * STRIPS, C, SW),
        "wq": both("wq"), "wk": both("wk"), "wv": both("wv"),
        "wf": both("wf").reshape(2, HEADS // 2, 2, DH, C).transpose(0, 2, 1, 3, 4).reshape(2, 2, C // 2, C),
        "bias_rows": np.stack([L0["sa_bf"], L0["ca_bf"], L0["ffn_b2"]]).reshape(1, 3 * C),
        "gains": np.stack([L0["ln_self_g"], L0["ln_cross_g"], L0["ln_out_g"]], axis=1),
        "shifts": np.stack([L0["ln_self_b"], L0["ln_cross_b"], L0["ln_out_b"]], axis=1),
        "b1": L0["ffn_b1"].reshape(FB, C).T,
        "w1": L0["ffn_w1"], "w2": L0["ffn_w2"],
        "convw": a["L1_conv_weight"].transpose(1, 2, 3, 0).reshape(C, TAPS * C),
        "bn": np.stack([a["L1_conv_gamma"], a["L1_conv_beta"]], axis=1),
        "consts": consts,
    }
    nc = bacc.Bacc("TRN2", target_bir_lowering=False, num_devices=1)
    maps, args = {}, {}
    for name, t in arrays.items():
        t = np.ascontiguousarray(t)
        maps["in_" + name] = t
        args[name] = nc.dram_tensor("in_" + name, t.shape, F32, kind="ExternalInput").ap()
    out = nc.dram_tensor("out_0", (IMAGES, C, H * W), F32, kind="ExternalOutput").ap()
    attention_conv(nc, out=out, **args)
    r = run_bass_kernel_spmd(nc, [maps], core_ids=[0])
    return r.results[0]["out_0"].reshape(IMAGES, C, H, W)
```

```python
from contextlib import ExitStack
from collections import namedtuple

import concourse.bass as bass
from concourse import mybir

ALU = mybir.AluOpType
ACT = mybir.ActivationFunctionType
AX = mybir.AxisListType
F32 = mybir.dt.float32
F16 = mybir.dt.float16
BF16 = mybir.dt.bfloat16

IMAGES, C, H, W = 8, 128, 64, 64
WIN = 8
TOK = WIN * WIN
HEADS = 8
DH = C // HEADS
STRIPS = H // WIN
SW = WIN * W
PAIRS = SW // (2 * TOK)
DOWN = 4
LH = H // DOWN
LT = LH * LH
LPAIRS = LT // (2 * TOK)
STRIDE = WIN // DOWN
KP = LH - STRIDE + WIN
DF = 512
FB = DF // C
VC = 66
MAP = W + 2
TAPS = 9
EPS = 1e-5
QS = DH ** -0.5
CHUNK = 1024
CHUNKS = H * W // CHUNK
PER = STRIPS // 2

Unit = namedtuple("Unit", "kind half par no pairs body crosses image i narrow")


def attention_conv(nc, x, wq, wk, wv, wf, bias_rows, columns, w1, w2, convw, consts, out):
    with ExitStack() as ctx:
        def sb(name, shape, dt=F32):
            return ctx.enter_context(nc.sbuf_tensor(name, shape, dt))

        def bank(name):
            return ctx.enter_context(nc.psum_tensor(name, [128, 512], F32))

        def sem(name):
            return ctx.enter_context(nc.semaphore(name))

        self_out = nc.dram_tensor("self_out", (IMAGES * STRIPS, C, SW), F32, kind="Internal").ap()
        ffn_out = nc.dram_tensor("ffn_out", (IMAGES, C, H * W), F32, kind="Internal").ap()

        wq_sb, wk_sb, wv_sb, wf_sb = (sb(n, [128, 2, C]) for n in ("wq_sb", "wk_sb", "wv_sb", "wf_sb"))
        w1_sb = sb("w1_sb", [128, DF])
        w2_sb = sb("w2_sb", [128, FB, C])
        columns_sb = sb("columns_sb", [128, 8 + FB])
        gain, shift = columns_sb[:, 0:3], columns_sb[:, 3:6]
        b1_sb, bn_sb = columns_sb[:, 6:6 + FB], columns_sb[:, 6 + FB:8 + FB]
        consts_sb = sb("consts_sb", [128, 2 * 128 + 12])
        ident, headmask, half_neg = consts_sb[:, 0:128], consts_sb[:, 128:132], consts_sb[:, 132:136]
        ones2_f, eps = consts_sb[0:2, 136:264], consts_sb[:, 264:268]
        convs = sb("convs", [128, TAPS, C], BF16)
        identb = sb("identb", [128, 128], BF16)
        ones2 = sb("ones2", [2, 128], F16)
        brow_f = sb("brow_f", [1, 3 * C])
        brow_hi = sb("brow_hi", [1, 3 * C], F16)
        brow_lo = sb("brow_lo", [1, 3 * C], F16)
        brow = sb("brow", [2, 3, C], F16)

        xself = sb("xself", [128, 2, SW])
        xcross = sb("xcross", [128, 2, SW])
        xpatch = sb("xpatch", [128, 2, SW])
        xlow = sb("xlow", [128, LT])
        qc_hi = sb("qc_hi", [128, 8 * TOK], F16)
        qc_lo = sb("qc_lo", [128, 8 * TOK], F16)
        qm_hi = sb("qm_hi", [128, 2, 8, 4, TOK], F16)
        qm_lo = sb("qm_lo", [128, 2, 8, 4, TOK], F16)
        ks_hi = sb("ks_hi", [128, 2, 8, 2, TOK], F16)
        ks_lo = sb("ks_lo", [128, 2, 8, 2, TOK], F16)
        vb_hi = sb("vb_hi", [128, 2, PAIRS * 4, VC], F16)
        vb_lo = sb("vb_lo", [128, 2, PAIRS * 4, VC], F16)
        negmax = sb("negmax", [128, 2, 8], BF16)
        prob = sb("prob", [128, 2, 512])
        prob_hi = sb("prob_hi", [128, 2, 512], F16)
        prob_lo = sb("prob_lo", [128, 2, 512], F16)
        rden = sb("rden", [128, 2, 4, 2])
        onorm = sb("onorm", [128, 2, PAIRS, C])
        oT = sb("oT", [128, SW])
        stats = sb("stats", [128, PAIRS, 6])
        mv = sb("mv", [128, PAIRS, 2])
        vareps = sb("vareps", [128, PAIRS])
        rstd = sb("rstd", [128, PAIRS])
        xn = sb("xn", [128, SW])
        stats2 = sb("stats2", [128, PAIRS, 6])
        mv2 = sb("mv2", [128, PAIRS, 2])
        vareps2 = sb("vareps2", [128, PAIRS])
        rstd2 = sb("rstd2", [128, PAIRS])
        xn2 = sb("xn2", [128, SW])
        xa = sb("xa", [128, 2, SW])
        colsum = sb("colsum", [128, SW // DOWN])
        low_sum = sb("low_sum", [128, STRIPS, 32])
        low_out = sb("low_out", [128, LT])
        kvpad = sb("kvpad", [128, KP, KP])
        xf = sb("xf", [128, SW])
        hid = sb("hid", [128, FB, SW])
        x2 = sb("x2", [128, 2, SW])
        smap = sb("smap", [128, MAP, MAP], BF16)
        yconv = sb("yconv", [128, IMAGES * H * W], F16)
        ystats = sb("ystats", [128, IMAGES * STRIPS, 6])
        bnv = sb("bnv", [128, 8])
        lastx = sb("lastx", [128, CHUNKS, CHUNK])
        lasty = sb("lasty", [128, 2, CHUNK])

        ps_proj, ps_hid, ps_max, ps_s, ps_o, ps_t, ps_y, ps_y2 = (
            bank(n) for n in ("ps_proj", "ps_hid", "ps_max", "ps_s", "ps_o", "ps_t", "ps_y", "ps_y2"))

        s_setup = sem("s_setup")
        s_bias = sem("s_bias")
        s_brow = sem("s_brow")
        s_xself_in = [sem("s_xself_in0"), sem("s_xself_in1")]
        s_xcross = [sem("s_xcross0"), sem("s_xcross1")]
        s_self_stored = [sem("s_self_stored0"), sem("s_self_stored1")]
        s_x2_stored = [sem("s_x2_stored0"), sem("s_x2_stored1")]
        s_last_in = [sem(f"s_last_in{q}") for q in range(CHUNKS)]
        s_last_out = [sem(f"s_last_out{q}") for q in range(CHUNKS)]
        s_prep_v = sem("s_prep_v")
        s_prep_a = sem("s_prep_a")
        s_prep_g = sem("s_prep_g")
        s_xpatch = sem("s_xpatch")
        s_rstd = sem("s_rstd")
        s_rstd2 = sem("s_rstd2")
        s_q = sem("s_q")
        s_k = sem("s_k")
        s_v = sem("s_v")
        s_proj_free = sem("s_proj_free")
        s_qhi = sem("s_qhi")
        s_qm_hi = sem("s_qm_hi")
        s_qm_lo = sem("s_qm_lo")
        s_khi = sem("s_khi")
        s_vhi = sem("s_vhi")
        s_ot = sem("s_ot")
        s_oT = sem("s_oT")
        s_resid = sem("s_resid")
        s_y = sem("s_y")
        s_stats = sem("s_stats")
        s_mv = sem("s_mv")
        s_var = sem("s_var")
        s_aggr = sem("s_aggr")
        s_gather = sem("s_gather")
        s_xn = sem("s_xn")
        s_xt = sem("s_xt")
        s_xt_out = sem("s_xt_out")
        s_max = sem("s_max")
        s_neg = sem("s_neg")
        s_s = sem("s_s")
        s_exp = sem("s_exp")
        s_prob = sem("s_prob")
        s_pv = sem("s_pv")
        s_rden = sem("s_rden")
        s_on = sem("s_on")
        s_hid = sem("s_hid")
        s_relu = sem("s_relu")
        s_y2 = sem("s_y2")
        s_stats2 = sem("s_stats2")
        s_mv2 = sem("s_mv2")
        s_var2 = sem("s_var2")
        s_xn2 = sem("s_xn2")
        s_xt2 = sem("s_xt2")
        s_x2 = sem("s_x2")
        s_sign = sem("s_sign")
        s_colsum = sem("s_colsum")
        s_pooled = sem("s_pooled")
        s_xlow = sem("s_xlow")
        s_kv0 = sem("s_kv0")
        s_kv1 = sem("s_kv1")
        s_kv = sem("s_kv")
        s_conv = sem("s_conv")
        s_yconv = sem("s_yconv")
        s_ystats = sem("s_ystats")
        s_bn = sem("s_bn")
        s_bnr = sem("s_bnr")
        s_bnab = sem("s_bnab")
        s_affine = sem("s_affine")
        s_sum = sem("s_sum")

        def pair_at(units, n):
            for u in units:
                if u is None or n < u.pairs:
                    return None if u is None else (u, n)
                n -= u.pairs

        def head(do, u):
            do("queries", u)
            do("gather", u)
            do("keys", u)
            do("masks_hi", u)
            do("keys_lo", u)
            do("masks_lo", u)
            do("values", u)
            do("take_values", u)
            do("rough", u, 0)
            do("scores", u, 0)
            do("rough", u, 1)

        ends_mixed = {
            "cross": ({0: dict(beside=("turn", "residual"), behind=("project",)),
                       1: dict(close=("apply",)), 2: dict(first=("spread",), behind=("hidden0",)),
                       3: dict(beside=("hidden1",), behind=("hidden2",))},
                      {0: dict(beside=("hidden3",), behind=("hidden4",)),
                       1: dict(close=("apply2",)), 2: dict(first=("out",)),
                       3: dict(beside=("conv",), behind=("conv_stats",))}),
            "self": ({2: dict(behind=("turn", "residual")), 3: dict(first=("project",), close=("apply",))},
                     {0: dict(first=("spread",)), 3: dict(beside=("pool",))})}
        ends_last = {
            "cross": (None, {0: dict(beside=("hidden3",), behind=("hidden4",)),
                             1: dict(close=("apply2",)), 2: dict(beside=("out",))}),
            "self": ({0: dict(beside=("turn", "residual"), behind=("project",)), 1: dict(close=("apply",)),
                      2: dict(first=("spread",)), 3: dict(first=("pool",))}, None)}
        ends_narrow = {
            "cross": ({0: dict(beside=("turn",), behind=("project",)),
                       1: dict(close=("apply",)), 2: dict(first=("spread",), behind=("hidden0",)),
                       3: dict(beside=("hidden1",), behind=("hidden2", "hidden3"))},
                      {0: dict(beside=("hidden4",)), 1: dict(first=("apply2",), behind=("out",)),
                       2: dict(beside=("conv",), behind=("conv_stats",))}),
            "self": ({0: dict(beside=("turn",), behind=("project",)), 1: dict(close=("apply",)),
                      2: dict(first=("spread",)), 3: dict(beside=("pool",))},
                     {})}
        starts_mixed = {0: (("queries",), ("masks_hi",)), 1: (("keys",), ("keys_lo", "masks_lo")),
                        2: ((), ("values", "take_values"))}
        starts_narrow = {0: ((), ("queries", "masks_hi")), 1: (("keys",), ("keys_lo", "masks_lo")),
                         2: ((), ("values", "take_values"))}

        def run_unit(do, u, older, before, after):
            narrow = u.narrow
            starts = starts_narrow if narrow else starts_mixed
            tables = ends_narrow if narrow else ends_last if after is None else ends_mixed

            def ends(k, place):
                for unit_of, distance in ((older, 1), (before, 0)):
                    if unit_of is None:
                        continue
                    for stage in tables[unit_of.kind][distance].get(k, {}).get(place, ()):
                        if stage not in ("conv", "conv_stats"):
                            do(stage, unit_of)
                        elif not narrow and not (type(unit_of.i) is int and unit_of.i + unit_of.half == 0):
                            do(stage, unit_of, unit_of.i * 2 + (unit_of.half - 1))
                        elif narrow and unit_of.half == 1:
                            do(stage, unit_of, unit_of.i)

            for k in range(u.pairs):
                nxt = pair_at((u, after), k + 1)
                over = pair_at((u, after), k + 2)
                before_it, behind_it = starts.get(k, ((), ())) if after else ((), ())
                if after and k == 0 and before is None:
                    do("gather", after)
                if nxt:
                    do("scores", *nxt)
                if over:
                    do("rough", *over)
                ends(k, "first")
                if after and k == 0 and before is not None:
                    do("gather", after)
                for stage in before_it:
                    do(stage, after)
                ends(k, "beside")
                do("weigh", u, k)
                ends(k, "close")
                for stage in behind_it:
                    do(stage, after)
                ends(k, "behind")
                if narrow and k == u.pairs - 1:
                    do("residual", u)

        def unit(kind, half, par, no, body, crosses, image, i, narrow):
            return Unit(kind, half, par, no, LPAIRS if kind == "low" else PAIRS, body, crosses, image, i,
                        narrow)

        def strips_of_image(do, fori, units_at):
            def body(i):
                units = units_at(i)
                earlier = units_at(i - 1)[-2:] if not (type(i) is int and i == 0) else [None, None]
                later = units_at(i + 1)[0] if not (type(i) is int and i == PER - 1) else None
                row = earlier + units + [later]
                for n in range(2, len(row) - 1):
                    run_unit(do, row[n], row[n - 2], row[n - 1], row[n + 1])

            body(0)
            with fori(0, PER - 2) as i:
                body(i + 1)
            body(PER - 1)
            return units_at(PER - 1)[-2:]

        def finish(do, older, last, low, nxt):
            if last.kind == "self":
                for stage in ("turn", "project", "apply", "spread", "pool"):
                    do(stage, last)
                ends = []
            elif low is not None:
                ends = ["residual", "project", "apply", "spread", "hidden0", "hidden1", "hidden2", "hidden3",
                        "hidden4"]
            else:
                do("turn", last)
                do("hidden4", older)
                do("project", last)
                do("apply2", older)
                do("conv", older, PER - 1)
                do("conv_stats", older, PER - 1)
                do("out", older)
                do("apply", last)
                do("conv", older, PER)
                do("conv_stats", older, PER)
                do("spread", last)
                do("conv", older, PER + 1)
                do("conv_stats", older, PER + 1)
                for stage in ("hidden0", "hidden1", "hidden2", "hidden3", "hidden4", "apply2", "out"):
                    do(stage, last)
                for strip in range(2 * PER - 2, STRIPS):
                    do("conv", last, strip)
                    do("conv_stats", last, strip)
                return

            def end():
                if ends:
                    stage = ends.pop(0)
                    do(stage, last)
                    if stage == "project":
                        do("conv", last._replace(crosses=last.crosses - 1), STRIPS - 3)
                    if stage == "spread":
                        do("conv_stats", last, STRIPS - 3)

            def start(stage, *pair):
                if nxt is not None:
                    do(stage, nxt, *pair)

            do("make_low", low)
            do("queries", low)
            if last.kind == "cross":
                do("turn", last)
            do("masks_hi", low)
            end()
            end()
            end()
            do("keys", low)
            do("keys_lo", low)
            do("masks_lo", low)
            end()
            do("values", low)
            do("take_values", low)
            end()
            do("rough", low, 0)
            end()
            do("scores", low, 0)
            do("rough", low, 1)
            end()
            do("scores", low, 1)
            start("queries")
            end()
            do("weigh", low, 0)
            start("keys")
            end()
            do("weigh", low, 1)
            do("turn", low)
            do("residual", low)
            start("masks_hi")
            start("keys_lo")
            if last.kind == "cross":
                do("apply2", last)
            do("project", low)
            start("values")
            if last.kind == "cross":
                do("out", last)
            do("apply", low)
            start("masks_lo")
            if last.kind == "cross":
                do("conv", last, STRIPS - 2)
            do("spread", low)
            do("pad_low", low)
            start("take_values")
            if last.kind == "cross":
                do("conv_stats", last, STRIPS - 2)
                do("conv", last, STRIPS - 1)
            start("rough", 0)
            start("scores", 0)
            start("rough", 1)
            if last.kind == "cross":
                do("conv_stats", last, STRIPS - 1)

        def walk(fori, do):
            per_image = 2 * STRIPS + 1

            def mixed(n):
                def units_at(i):
                    no = n * per_image + (i * 4 + (STRIPS + 1))
                    bc = n * PER + i
                    return [unit("self" if u % 2 == 0 else "cross", u // 2, u % 2, no + u,
                                 bc + PER if u % 2 == 0 else bc, bc * 2 + u // 2, n, i, False) for u in range(4)]
                return units_at

            def image(n, nxt):
                older, last = strips_of_image(do, fori, mixed(n))
                finish(do, older, last, unit("low", 0, 1, n * per_image + (3 * STRIPS + 1), n + 1,
                                             n * STRIPS + STRIPS, n, 0, False), nxt)

            def alone(i):
                return [unit("self", h, h, i * 2 + h, i, 0, 0, i, True) for h in range(2)]

            def last_alone(i):
                return [unit("cross", h, h, i * 2 + (h + STRIPS + 1 + (IMAGES - 1) * per_image),
                             i + (IMAGES - 1) * PER, (i + (IMAGES - 1) * PER) * 2 + h, IMAGES - 1, i, True)
                        for h in range(2)]

            head(do, alone(0)[0])
            older, last = strips_of_image(do, fori, alone)
            finish(do, older, last, unit("low", 0, 1, STRIPS, 0, 0, 0, 0, True), mixed(0)(0)[0])
            with fori(0, IMAGES - 2) as n:
                image(n, mixed(n + 1)(0)[0])
            image(IMAGES - 2, None)
            head(do, last_alone(0)[0])
            older, last = strips_of_image(do, fori, last_alone)
            finish(do, older, last, None, None)

        def out_follows(u):
            if u.kind == "low":
                return not u.narrow
            if u.kind == "self":
                return not u.narrow and type(u.i) is int and u.i == PER - 1 and u.half == 1
            return u.kind == "cross" and u.narrow

        def convolved(u):
            if u.narrow:
                return u.image * STRIPS + (2 * PER - 2 if type(u.i) is int and u.i * 2 + u.half == STRIPS - 1 else u.i)
            if type(u.i) is int and u.i == 0:
                return u.image * STRIPS
            return u.image * STRIPS + (u.i * 2 + (u.half - 1))

        def telling(stages):
            return lambda stage, *what: stages[stage](*what) if stage in stages else None

        def loads_after(u):
            if u.kind == "low" or (type(u.no) is int and u.no < 2):
                return None
            if type(u.i) is int and u.i == 0:
                return u.no - (1 if u.narrow else 2)
            return u.no - (1 if u.narrow else 3)

        def step(u):
            return PAIRS // u.pairs

        def pair_no(u, k):
            return u.no * PAIRS + k * step(u)

        def query_source(u):
            return xlow[:, :] if u.kind == "low" else (xself if u.kind == "self" else xcross)[:, u.half, :]

        def key_source(u):
            return xpatch[:, u.half, :] if u.kind == "cross" else query_source(u)

        def which(u):
            return 1 if u.kind == "cross" else 0

        block = ctx.enter_context(nc.Block())

        setup_loads = [
            (consts_sb[:, :], consts), (columns_sb[:, :], columns),
            (wq_sb[:, :, :], wq.rearrange("m c n -> c m n")), (wk_sb[:, :, :], wk.rearrange("m c n -> c m n")),
            (wv_sb[:, :, :], wv.rearrange("m c n -> c m n")),
            (hid[:, 0:3, :].rearrange("p a b -> p (a b)")[:, 0:TAPS * C], convw)]
        setup_loads += [(wf_sb[64 * h2:64 * h2 + 64, :, :], wf[h2].rearrange("m r n -> r m n")) for h2 in range(2)]
        setup_loads += [(w1_sb[:, :], w1), (w2_sb[:, :, :], w2.rearrange("(b f) n -> f b n", b=FB))]

        @block.sync
        def _(sp):
            sp.dma_start(brow_f[:, :], bias_rows).then_inc(s_bias, 16)
            for to, src in setup_loads[0::2]:
                sp.dma_start(to, src).then_inc(s_setup, 16)
            sp.wait_ge(s_prep_v, 2)
            for part, src in ((0, brow_hi), (1, brow_lo)):
                sp.dma_start(brow[part:part + 1, :, :], src[:, :].rearrange("p (a c) -> p a c", a=3)
                             ).then_inc(s_brow, 16)

            def load_tokens(u):
                strip = bass.ds(u.body * 2 + u.half, 1)
                if loads_after(u) is not None:
                    sp.wait_ge(s_resid, loads_after(u))
                if u.kind == "self":
                    sp.dma_start(xself[:, u.half, :], x[strip, :, :].rearrange("a c t -> (a c) t")
                                 ).then_inc(s_xself_in[u.half], 16)
                if u.kind == "cross":
                    sp.wait_ge(s_self_stored[u.half], u.body * 16 + 16)
                    sp.dma_start(xcross[:, u.half, :], self_out[strip, :, :].rearrange("a c t -> (a c) t")
                                 ).then_inc(s_xcross[u.half], 16)

            walk(nc.sync.Fori, telling({"queries": load_tokens}))

            for h in range(2):
                sp.wait_ge(s_x2_stored[h], 16 * IMAGES * PER)
            def chunk(dram, image, q):
                return dram[bass.ds(image, 1), :, q * CHUNK:(q + 1) * CHUNK].rearrange("a c t -> (a c) t")

            def load(image, q):
                sp.wait_ge(s_last_out[q], image * 16)
                sp.dma_start(lastx[:, q, :], chunk(ffn_out, image, q)).then_inc(s_last_in[q], 16)

            def store(image, q):
                sp.wait_ge(s_sum, image * CHUNKS + q + 1)
                sp.dma_start(chunk(out, image, q), lastx[:, q, :]).then_inc(s_last_out[q], 16)

            for q in range(CHUNKS):
                load(0, q)
            with nc.sync.Fori(0, IMAGES - 1) as i:
                for q in range(CHUNKS + 1):
                    if q < CHUNKS:
                        store(i, q)
                    if q:
                        load(i + 1, q - 1)
            for q in range(CHUNKS):
                store(IMAGES - 1, q)
            for q in range(CHUNKS):
                sp.wait_ge(s_last_out[q], 16 * IMAGES)

        @block.tensor
        def _(pe):
            mm = nc.tensor.matmul

            def project(u, kind):
                w = (wq_sb if kind == "q" else wk_sb)[:, which(u), :]
                src = (query_source(u) if kind == "q" else key_source(u)).rearrange(
                    "c (p w t) -> c p w t", w=2, t=TOK)
                n = u.pairs * TOK
                for g in range(2):
                    for win in range(2):
                        last = mm(ps_proj[64 * win:64 * win + 64, g * n:(g + 1) * n], w[:, 64 * g:64 * g + 64],
                                  src[:, :, win, :], start=True, stop=True, skip_group_check=True)
                last.then_inc(s_q if kind == "q" else s_k, 1)

            def project_q(u):
                if u.kind == "self":
                    pe.wait_ge(s_xself_in[u.half], u.body * 16 + 16)
                elif u.kind == "cross":
                    pe.wait_ge(s_xcross[u.half], u.body * 16 + 16)
                else:
                    pe.wait_ge(s_xlow, u.body + 1)
                pe.wait_ge(s_proj_free, u.no * 3)
                project(u, "q")

            def project_k(u):
                if u.kind == "cross":
                    pe.wait_ge(s_xpatch, u.body * 2 + (u.half + 1))
                pe.wait_ge(s_proj_free, u.no * 3 + 1)
                project(u, "k")

            def project_v(u):
                pe.wait_ge(s_proj_free, u.no * 3 + 2)
                src = key_source(u)
                for p in range(u.pairs):
                    last = mm(ps_proj[:, C * p:C * p + C], src[:, C * p:C * p + C], wv_sb[:, which(u), :],
                              start=True, stop=True, skip_group_check=True)
                last.then_inc(s_v, 1)

            def rough_scores(u, k):
                if k == 0:
                    pe.wait_ge(s_qm_hi, u.no + 1)
                    pe.wait_ge(s_khi, u.no + 1)
                for j in range(4):
                    a = (j // 2) * u.pairs + k
                    last = mm(ps_max[:, 128 * j:128 * j + 128],
                              qm_hi[:, u.par, a, 2 * (j % 2):2 * (j % 2) + 2, :].rearrange("p h t -> p (h t)"),
                              ks_hi[:, u.par, a, :, :].rearrange("p w t -> p (w t)"),
                              start=True, stop=True, skip_group_check=True)
                last.then_inc(s_max, step(u))

            def scores(u, k):
                ps = ps_s
                pe.wait_ge(s_exp, pair_no(u, k))
                if k == 0:
                    pe.wait_ge(s_qm_lo, u.no + 1)
                    pe.wait_ge(s_proj_free, u.no * 3 + 2)
                for g in range(2):
                    a = g * u.pairs + k
                    for n, (kk, qq) in enumerate(((ks_hi, qm_hi), (ks_hi, qm_lo), (ks_lo, qm_hi))):
                        mm(ps[:, 256 * g:256 * g + 256], kk[:, u.par, a, :, :].rearrange("p w t -> p (w t)"),
                           qq[:, u.par, a, :, :].rearrange("p h t -> p (h t)"),
                           start=(g == 0 and n == 0), stop=False, skip_group_check=True)
                pe.wait_ge(s_neg, pair_no(u, k) + step(u))
                for j in range(4):
                    for win in range(2):
                        last = mm(ps[64 * win:64 * win + 64, 128 * j:128 * j + 128],
                                  negmax[:, k % 2, 2 * j + win:2 * j + win + 1].to_broadcast([128, TOK]),
                                  identb[:, :], start=False, stop=True, skip_group_check=True)
                last.then_inc(s_s, step(u))

            def weigh(u, k):
                if k == 0:
                    pe.wait_ge(s_proj_free, u.no * 3 + 3)
                pe.wait_ge(s_prob, pair_no(u, k) + step(u))
                pe.wait_ge(s_on, pair_no(u, k))
                for j in range(4):
                    for n, (pp, vv) in enumerate(((prob_hi, vb_hi), (prob_lo, vb_hi), (prob_hi, vb_lo))):
                        last = mm(ps_o[:, VC * j:VC * j + VC], pp[:, k % 2, 128 * j:128 * j + 128],
                                  vv[:, u.par, 4 * k + j, :], start=(j == 0 and n == 0), stop=(n == 2),
                                  skip_group_check=True)
                last.then_inc(s_pv, step(u))

            def turn_heads(u):
                pe.wait_ge(s_on, u.no * PAIRS + PAIRS)
                pe.wait_ge(s_xt_out, u.no)
                pe.wait_ge(s_sign, u.crosses - 1 if out_follows(u) else u.crosses)
                for p in range(u.pairs):
                    last = mm(ps_t[:, C * p:C * p + C], onorm[:, u.par, p, :], ident[:, :], is_transpose=True,
                              start=True, stop=True, skip_group_check=True)
                last.then_inc(s_ot, 1)

            def residual(ps, pairs, src, bias):
                for p in range(pairs):
                    mm(ps[:, C * p:C * p + C], src[:, C * p:C * p + C], ident[:, :], is_transpose=True,
                       start=(p == 0), stop=False, skip_group_check=True)
                for p in range(pairs):
                    last = mm(ps[:, C * p:C * p + C], ones2[:, :], brow[:, bias, :], start=False, stop=False,
                              skip_group_check=True)
                return last

            def attention_residual(u):
                pe.wait_ge(s_xn, pair_no(u, 0))
                residual(ps_y, u.pairs, query_source(u), which(u)).then_inc(s_resid, 1)

            def project_out(u):
                pe.wait_ge(s_oT, u.no + 1)
                for p in range(u.pairs):
                    last = mm(ps_y[:, C * p:C * p + C], oT[:, C * p:C * p + C], wf_sb[:, which(u), :],
                              start=False, stop=True, skip_group_check=True)
                last.then_inc(s_y, 1)

            def turn_tokens(src, pairs, normalised, count_at, done):
                for p in range(pairs):
                    pe.wait_ge(normalised, count_at(p))
                    last = mm(ps_t[:, C * p:C * p + C], src[:, C * p:C * p + C], ident[:, :], is_transpose=True,
                              start=True, stop=True, skip_group_check=True)
                last.then_inc(done, 1)

            def spread(u):
                pe.wait_ge(s_sign, u.crosses - 1 if u.kind == "self" and out_follows(u) else u.crosses)
                turn_tokens(xn, u.pairs, s_xn, lambda p: pair_no(u, p) + step(u), s_xt)

            def hidden(u, b):
                if b == 0:
                    pe.wait_ge(s_xt_out, u.no + 1)
                    pe.wait_ge(s_yconv, convolved(u))
                pe.wait_ge(s_relu, u.crosses * FB + b)
                if b < FB:
                    mm(ps_hid[:, :], w1_sb[:, C * b:C * b + C], xf[:, :], start=True, stop=True,
                       skip_group_check=True).then_inc(s_hid, 1)
                if b == 0:
                    pe.wait_ge(s_xn2, u.crosses * PAIRS)
                    residual(ps_y2, PAIRS, xf, 2)
                else:
                    for p in range(PAIRS):
                        last = mm(ps_y2[:, C * p:C * p + C], hid[:, b - 1, C * p:C * p + C], w2_sb[:, b - 1, :],
                                  start=False, stop=(b == FB), skip_group_check=True)
                if b == FB:
                    last.then_inc(s_y2, 1)

            def turn_out(u):
                if not u.narrow and type(u.i) is int and u.i == PER - 1 and u.half == 0:
                    pe.wait_ge(s_xt_out, u.no + 2)
                turn_tokens(xn2, PAIRS, s_xn2, lambda p: u.crosses * PAIRS + p + 1, s_xt2)

            def conv(u, strip):
                pe.wait_ge(s_sign, u.image * STRIPS + (strip + (1 if type(strip) is int and strip == STRIPS - 1 else 2)))
                pe.wait_ge(s_relu, u.crosses * FB + FB)
                pe.wait_ge(s_yconv, u.image * STRIPS + strip)
                for t in range(TAPS):
                    dy, dx = t // 3, t % 3
                    last = mm(ps_hid[:, :].rearrange("p (r w) -> p r w", r=WIN), convs[:, t, :],
                              smap[:, bass.ds(strip * WIN + dy, WIN), dx:dx + W],
                              start=(t == 0), stop=(t == TAPS - 1), skip_group_check=True)
                last.then_inc(s_conv, 1)

            pe.wait_ge(s_setup, 16 * len(setup_loads))
            pe.wait_ge(s_brow, 16 * 2)
            pe.wait_ge(s_prep_v, 3)
            pe.wait_ge(s_prep_a, 1)
            pe.wait_ge(s_prep_g, 2)

            walk(nc.tensor.Fori, telling({
                "queries": project_q, "keys": project_k, "values": project_v, "rough": rough_scores,
                "scores": scores, "weigh": weigh, "turn": turn_heads, "residual": attention_residual,
                "project": project_out, "spread": spread,
                "hidden0": lambda u: hidden(u, 0), "hidden1": lambda u: hidden(u, 1),
                "hidden2": lambda u: hidden(u, 2), "hidden3": lambda u: hidden(u, 3),
                "hidden4": lambda u: hidden(u, 4),
                "out": turn_out, "conv": conv}))

        @block.scalar
        def _(act):
            activation = nc.scalar.activation

            def take_q(u):
                act.wait_ge(s_q, u.no + 1)
                a = 2 * u.pairs
                activation(qc_hi[:, 0:a * TOK], ps_proj[:, 0:a * TOK], ACT.Identity, scale=QS).then_inc(s_qhi, 1)

            def mask_q_hi(u):
                a = 2 * u.pairs
                act.wait_ge(s_qhi, u.no + 1)
                for h in range(4):
                    last = activation(qm_hi[:, u.par, 0:a, h, :],
                                      qc_hi[:, 0:a * TOK].rearrange("p (a t) -> p a t", a=a), ACT.Identity,
                                      scale=headmask[:, h:h + 1])
                last.then_inc(s_qm_hi, 1)

            def take_k(u):
                act.wait_ge(s_k, u.no + 1)
                a = 2 * u.pairs
                for win in range(2):
                    r = slice(64 * win, 64 * win + 64)
                    last = activation(ks_hi[r, u.par, 0:a, win, :],
                                      ps_proj[r, 0:a * TOK].rearrange("p (a t) -> p a t", a=a), ACT.Identity)
                last.then_inc(s_khi, 1)

            def take_v(u):
                act.wait_ge(s_v, u.no + 1)
                a = 4 * u.pairs
                for win in range(2):
                    r = slice(64 * win, 64 * win + 64)
                    last = activation(vb_hi[r, u.par, 0:a, 32 * win:32 * win + 32],
                                      ps_proj[r, 0:a * 32].rearrange("p (a t) -> p a t", a=a), ACT.Identity)
                last.then_inc(s_vhi, 1)

            def exponentials(u, k):
                act.wait_ge(s_s, pair_no(u, k) + step(u))
                activation(prob[:, k % 2, :], ps_s[:, :], ACT.Exp)
                activation(prob_hi[:, k % 2, :], ps_s[:, :], ACT.Exp).then_inc(s_exp, step(u))

            def take_turned(u):
                act.wait_ge(s_ot, u.no + 1)
                n = u.pairs * C
                src = ps_t[:, 0:n].rearrange("p (a h t) -> p a h t", h=2, t=TOK)
                to = oT[:, 0:n].rearrange("p (a w t) -> p a w t", w=2, t=TOK)
                for win in range(2):
                    for h2 in range(2):
                        last = activation(to[64 * h2:64 * h2 + 64, :, win, :], src[64 * win:64 * win + 64, :, h2, :],
                                          ACT.Identity)
                last.then_inc(s_oT, 1)

            def take_output(u):
                act.wait_ge(s_xt, u.no + 1)
                if u.kind == "self":
                    act.wait_ge(s_self_stored[u.half], u.body * 16)
                    act.wait_ge(s_colsum, u.body * 2 + u.half)
                    to = xa[:, u.half, :]
                elif u.kind == "cross":
                    to = xf[:, :]
                else:
                    act.wait_ge(s_kv0, u.body)
                    to = low_out[:, :]
                m = which(u)
                activation(to, ps_t[:, 0:u.pairs * C], ACT.Identity, bias=shift[:, m:m + 1],
                           scale=gain[:, m:m + 1]).then_inc(s_xt_out, 1)

            def store_self(u):
                act.wait_ge(s_xt_out, u.no + 1)
                act.dma_start(self_out[bass.ds(u.body * 2 + u.half, 1), :, :].rearrange("a c t -> (a c) t"),
                              xa[:, u.half, :]).then_inc(s_self_stored[u.half], 16)

            def take_hidden(u, b):
                act.wait_ge(s_hid, u.crosses * FB + b + 1)
                activation(hid[:, b, :], ps_hid[:, :], ACT.Relu, bias=b1_sb[:, b:b + 1]).then_inc(s_relu, 1)

            def take_out(u):
                act.wait_ge(s_xt2, u.crosses + 1)
                act.wait_ge(s_x2_stored[u.half], u.body * 16)
                src = ps_t[:, :].rearrange("p (v r w) -> p v r w", v=WIN, r=WIN)
                activation(x2[:, u.half, :].rearrange("p (r v w) -> p v r w", r=WIN, v=WIN), src, ACT.Identity,
                           bias=shift[:, 2:3], scale=gain[:, 2:3]).then_inc(s_x2, 1)
                act.wait_ge(s_conv, u.image * STRIPS)
                rows = smap[:, bass.ds(u.i * 2 * WIN + (u.half * WIN + 1), WIN), 1:1 + W]
                activation(rows.rearrange("p r (v w) -> p v r w", v=WIN), src, ACT.Sign,
                           bias=shift[:, 2:3], scale=gain[:, 2:3]).then_inc(s_sign, 1)
                act.wait_ge(s_x2, u.crosses + 1)
                act.dma_start(ffn_out[bass.ds(u.image, 1), :, bass.ds(u.i * 2 * SW + u.half * SW, SW)
                                      ].rearrange("a c t -> (a c) t"),
                              x2[:, u.half, :]).then_inc(s_x2_stored[u.half], 16)

            def take_conv(u, strip):
                act.wait_ge(s_conv, u.image * STRIPS + (strip + 1))
                activation(yconv[:, bass.ds(u.image * H * W + strip * SW, SW)], ps_hid[:, :], ACT.Identity
                           ).then_inc(s_yconv, 1)

            for to, src in setup_loads[1::2]:
                act.dma_start(to, src).then_inc(s_setup, 16)
            act.wait_ge(s_setup, 16 * len(setup_loads))
            activation(convs[:, :, :].rearrange("p a b -> p (a b)"),
                       hid[:, 0:3, :].rearrange("p a b -> p (a b)")[:, 0:TAPS * C], ACT.Sign).then_inc(s_prep_a, 1)
            act.wait_ge(s_prep_v, 3)
            act.wait_ge(s_prep_g, 2)
            act.wait_ge(s_prep_a, 1)

            walk(nc.scalar.Fori, telling({
                "queries": take_q, "masks_hi": mask_q_hi, "keys": take_k, "take_values": take_v, "scores": exponentials, "turn": take_turned,
                "spread": take_output, "hidden0": lambda u: take_hidden(u, 0),
                "hidden1": lambda u: take_hidden(u, 1), "hidden2": lambda u: take_hidden(u, 2),
                "hidden3": lambda u: take_hidden(u, 3), "pool": store_self, "out": take_out,
                "conv": take_conv}))

            act.wait_ge(s_bnab, 3)
            with nc.scalar.Fori(0, IMAGES) as i:
                for q in range(CHUNKS):
                    act.wait_ge(s_sum, i * CHUNKS + (q - 1) if q else i * CHUNKS)
                    activation(lasty[:, q % 2, :], yconv[:, bass.ds(i * H * W + q * CHUNK, CHUNK)], ACT.Identity,
                               bias=bnv[:, 6:7], scale=bnv[:, 4:5]).then_inc(s_affine, 1)

        @block.vector
        def _(dve):
            v = nc.vector

            def split_q(u):
                dve.wait_ge(s_qhi, u.no + 1)
                a = 2 * u.pairs
                v.scalar_tensor_tensor(out=qc_lo[:, 0:a * TOK], in0=ps_proj[:, 0:a * TOK], scalar=QS,
                                       in1=qc_hi[:, 0:a * TOK], op0=ALU.mult, op1=ALU.subtract
                                       ).then_inc(s_proj_free, 1)

            def mask_q_lo(u):
                a = 2 * u.pairs
                dve.wait_ge(s_proj_free, u.no * 3 + 1)
                for h in range(4):
                    last = v.tensor_scalar(qm_lo[:, u.par, 0:a, h, :],
                                           qc_lo[:, 0:a * TOK].rearrange("p (a t) -> p a t", a=a),
                                           headmask[:, h:h + 1], None, ALU.mult)
                last.then_inc(s_qm_lo, 1)

            def split_k(u):
                dve.wait_ge(s_khi, u.no + 1)
                a = 2 * u.pairs
                for win in range(2):
                    r = slice(64 * win, 64 * win + 64)
                    last = v.tensor_tensor(ks_lo[r, u.par, 0:a, win, :],
                                           ps_proj[r, 0:a * TOK].rearrange("p (a t) -> p a t", a=a),
                                           ks_hi[r, u.par, 0:a, win, :], ALU.subtract)
                last.then_inc(s_proj_free, 1)

            def split_v(u):
                dve.wait_ge(s_vhi, u.no + 1)
                a = 4 * u.pairs
                for win in range(2):
                    r = slice(64 * win, 64 * win + 64)
                    last = v.tensor_tensor(vb_lo[r, u.par, 0:a, 32 * win:32 * win + 32],
                                           ps_proj[r, 0:a * 32].rearrange("p (a t) -> p a t", a=a),
                                           vb_hi[r, u.par, 0:a, 32 * win:32 * win + 32], ALU.subtract)
                last.then_inc(s_proj_free, 1)

            def maxima(u, k):
                dve.wait_ge(s_max, pair_no(u, k) + step(u))
                v.tensor_reduce(negmax[:, k % 2, :], ps_max[:, :].rearrange("p (a t) -> p a t", t=TOK), AX.X,
                                ALU.max, negate=True).then_inc(s_neg, step(u))

            def normalise(u, k):
                dve.wait_ge(s_pv, pair_no(u, k) + step(u))
                blocks = ps_o[:, 0:4 * VC].rearrange("p (j c) -> p j c", j=4)
                v.reciprocal(rden[:, k % 2, :, :], blocks[:, :, 64:66]).then_inc(s_rden, step(u))
                dve.wait_ge(s_rden, pair_no(u, k) + step(u))
                for h2 in range(2):
                    r = slice(64 * h2, 64 * h2 + 64)
                    last = v.tensor_tensor(
                        onorm[r, u.par, k, :].rearrange("p (w j d) -> p j w d", w=2, j=4),
                        blocks[r, :, 0:64].rearrange("p j (w h d) -> p j w h d", w=2, h=2)[:, :, :, h2, :],
                        rden[r, k % 2, :, :].unsqueeze(3).to_broadcast([64, 4, 2, DH]), ALU.mult)
                last.then_inc(s_on, step(u))

            def norm_stats(ps, to, mean_var, pairs, done, count, stats_done, mv_done):
                dve.wait_ge(done, count)
                for p in range(pairs):
                    last = v.bn_stats(to[:, p, :], ps[:, C * p:C * p + C])
                last.then_inc(stats_done, 1)
                dve.wait_ge(stats_done, count)
                dve.sem_inc(s_aggr, 1)
                for p in range(pairs):
                    last = v.bn_aggr(mean_var[:, p, :], to[:, p, :])
                last.then_inc(mv_done, 1)

            def norm_apply(ps, to, mean_var, factor, pairs, count, rstd_done, done, by):
                dve.wait_ge(rstd_done, count)
                for p in range(pairs):
                    v.tensor_scalar(to[:, C * p:C * p + C], ps[:, C * p:C * p + C], mean_var[:, p, 0:1],
                                    factor[:, p:p + 1], ALU.subtract, ALU.mult).then_inc(done, by)

            def stats_of(u):
                norm_stats(ps_y, stats, mv, u.pairs, s_y, u.no + 1, s_stats, s_mv)

            def apply_to(u):
                norm_apply(ps_y, xn, mv, rstd, u.pairs, u.no + 1, s_rstd, s_xn, step(u))

            def stats2_of(u):
                norm_stats(ps_y2, stats2, mv2, PAIRS, s_y2, u.crosses + 1, s_stats2, s_mv2)

            def apply2_to(u):
                norm_apply(ps_y2, xn2, mv2, rstd2, PAIRS, u.crosses + 1, s_rstd2, s_xn2, 1)

            def pool(u):
                strip = u.body * 2 + u.half
                dve.wait_ge(s_xt_out, u.no + 1)
                dve.wait_ge(s_pooled, strip)
                v.tensor_reduce(colsum[:, :], xa[:, u.half, :].rearrange("p (a f) -> p a f", f=DOWN), AX.X,
                                ALU.add).then_inc(s_colsum, 1)
                dve.wait_ge(s_colsum, strip + 1)
                v.tensor_reduce(low_sum[:, bass.ds(u.i * 2 + u.half, 1), :].rearrange("p a (w c) -> p (a w) c", c=2),
                                colsum[:, :].rearrange("p (w r c) -> p w c r", r=DOWN, c=2), AX.X,
                                ALU.add).then_inc(s_pooled, 1)

            def make_low(low):
                dve.wait_ge(s_pooled, low.body * STRIPS + STRIPS)
                q = LH // WIN
                for wi in range(q):
                    last = v.tensor_scalar(
                        xlow[:, :].rearrange("p (a b s t) -> p a b s t", a=q, b=q, s=4)[:, wi, :, :, :],
                        low_sum[:, 4 * wi:4 * wi + 4, :].rearrange("p s (b t) -> p b s t", b=q),
                        1.0 / (DOWN * DOWN), None, ALU.mult)
                last.then_inc(s_xlow, 1)

            def pad_low(low):
                dve.wait_ge(s_xt_out, low.no + 1)
                dve.wait_ge(s_xpatch, low.body * STRIPS)
                q = LH // WIN
                for wi in range(q):
                    for wj in range(q):
                        src = low_out[:, :].rearrange("p (a s v r c) -> p a s v r c", a=q * q, s=4, v=4, r=2)
                        for r in range(2):
                            rows = kvpad[:, WIN * wi:WIN * wi + WIN, WIN * wj:WIN * wj + WIN]
                            last = v.tensor_copy(
                                rows.rearrange("p (s r) (v c) -> p s r v c", r=2, c=2)[:, :, r, :, :],
                                src[:, q * wi + wj, :, :, r, :])
                last.then_inc(s_kv0, 1)
                dve.wait_ge(s_kv0, low.body + 1)
                v.tensor_copy(kvpad[:, 0:LH, LH:KP], kvpad[:, 0:LH, 0:KP - LH]).then_inc(s_kv1, 1)
                dve.wait_ge(s_kv1, low.body + 1)
                v.tensor_copy(kvpad[:, LH:KP, :], kvpad[:, 0:KP - LH, :]).then_inc(s_kv, 1)

            def conv_stats(u, strip):
                dve.wait_ge(s_yconv, u.image * STRIPS + (strip + 1))
                v.bn_stats(ystats[:, bass.ds(u.image * STRIPS + strip, 1), :].rearrange("p a b -> p (a b)"),
                           yconv[:, bass.ds(u.image * H * W + strip * SW, SW)]).then_inc(s_ystats, 1)

            v.memset(ks_hi[:, :, :, :, :], 0.0)
            v.memset(ks_lo[:, :, :, :, :], 0.0)
            dve.wait_ge(s_bias, 16)
            v.tensor_copy(brow_hi[:, :], brow_f[:, :]).then_inc(s_prep_v, 1)
            dve.wait_ge(s_prep_v, 1)
            v.tensor_tensor(brow_lo[:, :], brow_f[:, :], brow_hi[:, :], ALU.subtract).then_inc(s_prep_v, 1)
            dve.wait_ge(s_setup, 16 * len(setup_loads))
            v.tensor_copy(ones2[:, :], ones2_f[:, :])
            v.tensor_copy(identb[:, :], ident[:, :]).then_inc(s_prep_v, 1)
            dve.wait_ge(s_prep_v, 3)
            dve.wait_ge(s_prep_g, 2)

            walk(nc.vector.Fori, telling({
                "queries": split_q, "masks_lo": mask_q_lo, "keys_lo": split_k,
                "take_values": split_v, "rough": maxima, "weigh": normalise, "project": stats_of,
                "apply": apply_to, "hidden4": stats2_of, "apply2": apply2_to, "pool": pool, "make_low": make_low,
                "pad_low": pad_low, "conv_stats": conv_stats}))

            dve.wait_ge(s_ystats, IMAGES * STRIPS)
            v.bn_aggr(bnv[:, 0:2], ystats[:, :, :].rearrange("p a b -> p (a b)")).then_inc(s_bn, 1)
            dve.wait_ge(s_bnr, 2)
            v.tensor_tensor(bnv[:, 4:5], bnv[:, 3:4], bn_sb[:, 0:1], ALU.mult).then_inc(s_bnab, 1)
            dve.wait_ge(s_bnab, 1)
            v.tensor_tensor(bnv[:, 5:6], bnv[:, 0:1], bnv[:, 4:5], ALU.mult).then_inc(s_bnab, 1)
            dve.wait_ge(s_bnab, 2)
            v.tensor_tensor(bnv[:, 6:7], bn_sb[:, 1:2], bnv[:, 5:6], ALU.subtract).then_inc(s_bnab, 1)
            with nc.vector.Fori(0, IMAGES) as i:
                for q in range(CHUNKS):
                    dve.wait_ge(s_last_in[q], i * 16 + 16)
                    dve.wait_ge(s_affine, i * CHUNKS + q + 1)
                    v.tensor_tensor(lastx[:, q, :], lastx[:, q, :], lasty[:, q % 2, :], ALU.add).then_inc(s_sum, 1)

        @block.gpsimd
        def _(pool):
            g = nc.gpsimd

            def inv_sqrt(var, var_eps, to, pairs, count, mv_done, var_done, rstd_done):
                pool.wait_ge(mv_done, count)
                g.tensor_tensor(var_eps[:, 0:pairs], var[:, 0:pairs, 1], eps[:, 0:pairs], ALU.add
                                ).then_inc(var_done, 1)
                pool.wait_ge(var_done, count)
                g.tensor_tensor(to[:, 0:pairs], var_eps[:, 0:pairs], half_neg[:, 0:pairs], ALU.pow
                                ).then_inc(rstd_done, 1)

            def split_prob(u, k):
                pool.wait_ge(s_exp, pair_no(u, k) + step(u))
                g.tensor_tensor(prob_lo[:, k % 2, :], prob[:, k % 2, :], prob_hi[:, k % 2, :], ALU.subtract
                                ).then_inc(s_prob, step(u))

            def rstd_of(u):
                inv_sqrt(mv, vareps, rstd, u.pairs, u.no + 1, s_mv, s_var, s_rstd)

            def rstd2_of(u):
                inv_sqrt(mv2, vareps2, rstd2, PAIRS, u.crosses + 1, s_mv2, s_var2, s_rstd2)

            def gather(u):
                if u.kind != "cross":
                    return
                pool.wait_ge(s_kv, u.image + 1)
                pool.wait_ge(s_resid, loads_after(u))
                pool.sem_inc(s_gather, 1)
                rows = kvpad[:, bass.ds(u.i * 2 * STRIDE + u.half * STRIDE, WIN), :]
                for win in range(STRIPS):
                    last = g.tensor_copy(
                        xpatch[:, u.half, TOK * win:TOK * win + TOK].rearrange("p (r c) -> p r c", r=WIN),
                        rows[:, :, STRIDE * win:STRIDE * win + WIN])
                last.then_inc(s_xpatch, 1)

            g.memset(smap[:, :, :], 0.0)
            g.memset(vb_lo[:, :, :, :], 0.0)
            g.memset(vb_hi[:, :, :, :], 0.0).then_inc(s_prep_g, 1)
            pool.wait_ge(s_prep_g, 1)
            for win in range(2):
                last = g.memset(vb_hi[64 * win:64 * win + 64, :, :, 64 + win:65 + win], 1.0)
            last.then_inc(s_prep_g, 1)
            pool.wait_ge(s_setup, 16 * len(setup_loads))

            walk(nc.gpsimd.Fori, telling({"gather": gather, "scores": split_prob, "project": rstd_of, "hidden4": rstd2_of}))
            pool.wait_ge(s_bn, 1)
            g.tensor_tensor(bnv[:, 2:3], bnv[:, 1:2], eps[:, 0:1], ALU.add).then_inc(s_bnr, 1)
            pool.wait_ge(s_bnr, 1)
            g.tensor_tensor(bnv[:, 3:4], bnv[:, 2:3], half_neg[:, 0:1], ALU.pow).then_inc(s_bnr, 1)


def kernel(**inputs):
    import numpy as np
    import concourse.bacc as bacc
    from concourse.bass_utils import run_bass_kernel_spmd

    a = {k: np.asarray(t) for k, t in inputs.items()}
    L0 = {k[len("L0_conv_"):]: t for k, t in a.items() if k.startswith("L0_conv_")}
    both = lambda name: np.stack([L0["sa_" + name], L0["ca_" + name]])
    consts = np.zeros((128, 268), np.float32)
    consts[:, 0:128] = np.eye(128)
    for h in range(4):
        for win in range(2):
            consts[win * 64 + h * DH:win * 64 + h * DH + DH, 128 + h] = 1.0
    consts[:, 132:136] = -0.5
    consts[:, 136:264] = 1.0
    consts[:, 264:268] = EPS
    arrays = {
        "x": a["x"].reshape(IMAGES, C, STRIPS, WIN, W // WIN, WIN).transpose(0, 2, 1, 4, 3, 5
                                                                             ).reshape(IMAGES * STRIPS, C, SW),
        "wq": both("wq"), "wk": both("wk"), "wv": both("wv"),
        "wf": both("wf").reshape(2, HEADS // 2, 2, DH, C).transpose(2, 0, 1, 3, 4).reshape(2, 2, C // 2, C),
        "bias_rows": np.stack([L0["sa_bf"], L0["ca_bf"], L0["ffn_b2"]]).reshape(1, 3 * C),
        "columns": np.concatenate([
            np.stack([L0["ln_self_g"], L0["ln_cross_g"], L0["ln_out_g"]], axis=1),
            np.stack([L0["ln_self_b"], L0["ln_cross_b"], L0["ln_out_b"]], axis=1),
            L0["ffn_b1"].reshape(FB, C).T,
            np.stack([a["L1_conv_gamma"], a["L1_conv_beta"]], axis=1)], axis=1),
        "w1": L0["ffn_w1"], "w2": L0["ffn_w2"],
        "convw": a["L1_conv_weight"].transpose(1, 2, 3, 0).reshape(C, TAPS * C),
        "consts": consts,
    }
    nc = bacc.Bacc("TRN2", target_bir_lowering=False, num_devices=1)
    maps, args = {}, {}
    for name, t in arrays.items():
        t = np.ascontiguousarray(t)
        maps["in_" + name] = t
        args[name] = nc.dram_tensor("in_" + name, t.shape, F32, kind="ExternalInput").ap()
    out = nc.dram_tensor("out_0", (IMAGES, C, H * W), F32, kind="ExternalOutput").ap()
    attention_conv(nc, out=out, **args)
    r = run_bass_kernel_spmd(nc, [maps], core_ids=[0])
    return r.results[0]["out_0"].reshape(IMAGES, C, H, W)
```
